# Optimizing a Trainium2 kernel written in Bass

```python
import numpy as np
import jax
import jax.numpy as jnp

def _softmax(x, axis=-1):
    return jax.nn.softmax(x, axis=axis)

def _gelu(x):
    return jax.nn.gelu(x, approximate=True)

def _silu(x):
    return jax.nn.silu(x)

def _sigmoid(x):
    return jax.nn.sigmoid(x)

def _layernorm(x, axis=-1, eps=1e-05):
    m = jnp.mean(x, axis=axis, keepdims=True)
    v = jnp.var(x, axis=axis, keepdims=True)
    return (x - m) / jnp.sqrt(v + eps)

def _scatter_add(tgt, idx, src, axis=0):
    return tgt.at[idx].add(src)

def _segment_sum(src, seg, n):
    return jax.ops.segment_sum(src, seg, n)
kernel_name = 'mk_prb_d1_jaxref_r4_004917'

def setup_inputs(seed: int=0):
    np.random.seed(seed)
    _w = jnp.asarray

    def _L0_attn_setup():
        import jax, jax.numpy as jnp
        from jax import lax
        import numpy as np
        DIM = 256
        HID = 384
        K = 4
        C_CONST = 8.0

        def _hawk_forward(x, Wg, Wi, conv_w, conv_b, lru_Wi, lru_bi, lru_Wg, lru_bg, lam, Wo):
            H = Wg.shape[0]
            k = conv_w.shape[-1]
            gate = jnp.einsum('bsd,hd->bsh', x, Wg)
            u = jnp.einsum('bsd,hd->bsh', x, Wi)
            y = lax.conv_general_dilated(u.transpose(0, 2, 1), conv_w, window_strides=(1,), padding=[(k - 1, 0)], dimension_numbers=('NCH', 'OIH', 'NCH'), feature_group_count=H) + conv_b[None, :, None]
            y = y.transpose(0, 2, 1)
            ig = jax.nn.sigmoid(jnp.einsum('bsh,gh->bsg', y, lru_Wi) + lru_bi)
            rg = jax.nn.sigmoid(jnp.einsum('bsh,gh->bsg', y, lru_Wg) + lru_bg)
            alpha = jnp.exp(-C_CONST * jax.nn.softplus(lam) * rg)
            beta = jnp.sqrt(1.0 - alpha ** 2 + 1e-06)
            xbeta = beta * ig * y

            def combine(c1, c2):
                a1, b1 = c1
                a2, b2 = c2
                return (a1 * a2, a2 * b1 + b2)
            _, h = lax.associative_scan(combine, (alpha, xbeta), axis=1)
            return jnp.einsum('bsh,dh->bsd', jax.nn.gelu(gate, approximate=False) * h, Wo)
        key = jax.random.key(seed)
        ks = jax.random.split(key, 12)
        d, h = (DIM, HID)
        x = jax.random.normal(ks[0], (4, 1024, d), dtype=jnp.float32)
        Wg = jax.random.normal(ks[1], (h, d), dtype=jnp.float32) * d ** (-0.5)
        Wi = jax.random.normal(ks[2], (h, d), dtype=jnp.float32) * d ** (-0.5)
        conv_w = jax.random.normal(ks[3], (h, 1, K), dtype=jnp.float32) * (1.0 / K) ** 0.5
        conv_b = jax.random.normal(ks[4], (h,), dtype=jnp.float32) * 0.02
        lru_Wi = jax.random.normal(ks[5], (h, h), dtype=jnp.float32) * h ** (-0.5)
        lru_bi = jnp.zeros((h,), dtype=jnp.float32)
        lru_Wg = jax.random.normal(ks[6], (h, h), dtype=jnp.float32) * h ** (-0.5)
        lru_bg = jnp.zeros((h,), dtype=jnp.float32)
        lam = jnp.linspace(-4.323, -9.0, h, dtype=jnp.float32)
        Wo = jax.random.normal(ks[7], (d, h), dtype=jnp.float32) * h ** (-0.5)
        return {'x': x, 'Wg': Wg, 'Wi': Wi, 'conv_w': conv_w, 'conv_b': conv_b, 'lru_Wi': lru_Wi, 'lru_bi': lru_bi, 'lru_Wg': lru_Wg, 'lru_bg': lru_bg, 'lam': lam, 'Wo': Wo}
    _L0_attn_in = _L0_attn_setup()

    def _L0_ffn_setup():
        import jax, jax.numpy as jnp
        import numpy as np
        DIM = 256

        def _reference_tuple_inner(x, W_r, W_k, W_v, mu_r, mu_k):
            B, T, C = x.shape
            x_prev = jnp.concatenate([jnp.zeros((B, 1, C), x.dtype), x[:, :-1, :]], axis=1)
            xr = mu_r * x + (1.0 - mu_r) * x_prev
            xk = mu_k * x + (1.0 - mu_k) * x_prev
            r = jax.nn.sigmoid(jnp.einsum('btc,dc->btd', xr, W_r))
            k = jnp.einsum('btc,dc->btd', xk, W_k)
            k_act = jnp.square(jax.nn.relu(k))
            out = r * jnp.einsum('btc,dc->btd', k_act, W_v)
            new_state = x[:, -1, :]
            return (out, new_state)
        key = jax.random.key(seed)
        ks = jax.random.split(key, 6)
        B, T, C = (8, 512, DIM)
        x = jax.random.normal(ks[0], (B, T, C), dtype=jnp.float32)
        s = 1.0 / np.sqrt(C)
        W_r = jax.random.uniform(ks[1], (C, C), jnp.float32, -s, s)
        W_k = jax.random.uniform(ks[2], (C, C), jnp.float32, -s, s)
        W_v = jax.random.uniform(ks[3], (C, C), jnp.float32, -s, s)
        mu_r = jax.random.uniform(ks[4], (C,), jnp.float32)
        mu_k = jax.random.uniform(ks[5], (C,), jnp.float32)
        return {'x': x, 'W_r': W_r, 'W_k': W_k, 'W_v': W_v, 'mu_r': mu_r, 'mu_k': mu_k}
    _L0_ffn_in = _L0_ffn_setup()
    _d = {'L0_attn_x': _L0_attn_in['x'], 'L0_attn_Wg': _L0_attn_in['Wg'], 'L0_attn_Wi': _L0_attn_in['Wi'], 'L0_attn_conv_w': _L0_attn_in['conv_w'], 'L0_attn_conv_b': _L0_attn_in['conv_b'], 'L0_attn_lru_Wi': _L0_attn_in['lru_Wi'], 'L0_attn_lru_bi': _L0_attn_in['lru_bi'], 'L0_attn_lru_Wg': _L0_attn_in['lru_Wg'], 'L0_attn_lru_bg': _L0_attn_in['lru_bg'], 'L0_attn_lam': _L0_attn_in['lam'], 'L0_attn_Wo': _L0_attn_in['Wo'], 'L0_ffn_W_r': _L0_ffn_in['W_r'], 'L0_ffn_W_k': _L0_ffn_in['W_k'], 'L0_ffn_W_v': _L0_ffn_in['W_v'], 'L0_ffn_mu_r': _L0_ffn_in['mu_r'], 'L0_ffn_mu_k': _L0_ffn_in['mu_k']}
    _x0 = _d['L0_attn_x']
    _d['L0_attn_x'] = jax.random.normal(jax.random.fold_in(jax.random.key(seed), 1), (8, 1024, 256), dtype=_x0.dtype)
    del _x0
    return _d

def reference(L0_attn_x, L0_attn_Wg, L0_attn_Wi, L0_attn_conv_w, L0_attn_conv_b, L0_attn_lru_Wi, L0_attn_lru_bi, L0_attn_lru_Wg, L0_attn_lru_bg, L0_attn_lam, L0_attn_Wo, L0_ffn_W_r, L0_ffn_W_k, L0_ffn_W_v, L0_ffn_mu_r, L0_ffn_mu_k):

    def _L0_attn_ref(x, Wg, Wi, conv_w, conv_b, lru_Wi, lru_bi, lru_Wg, lru_bg, lam, Wo):
        import jax, jax.numpy as jnp
        from jax import lax
        import numpy as np
        DIM = 256
        HID = 384
        K = 4
        C_CONST = 8.0

        def _hawk_forward(x, Wg, Wi, conv_w, conv_b, lru_Wi, lru_bi, lru_Wg, lru_bg, lam, Wo):
            H = Wg.shape[0]
            k = conv_w.shape[-1]
            gate = jnp.einsum('bsd,hd->bsh', x, Wg)
            u = jnp.einsum('bsd,hd->bsh', x, Wi)
            y = lax.conv_general_dilated(u.transpose(0, 2, 1), conv_w, window_strides=(1,), padding=[(k - 1, 0)], dimension_numbers=('NCH', 'OIH', 'NCH'), feature_group_count=H) + conv_b[None, :, None]
            y = y.transpose(0, 2, 1)
            ig = jax.nn.sigmoid(jnp.einsum('bsh,gh->bsg', y, lru_Wi) + lru_bi)
            rg = jax.nn.sigmoid(jnp.einsum('bsh,gh->bsg', y, lru_Wg) + lru_bg)
            alpha = jnp.exp(-C_CONST * jax.nn.softplus(lam) * rg)
            beta = jnp.sqrt(1.0 - alpha ** 2 + 1e-06)
            xbeta = beta * ig * y

            def combine(c1, c2):
                a1, b1 = c1
                a2, b2 = c2
                return (a1 * a2, a2 * b1 + b2)
            _, h = lax.associative_scan(combine, (alpha, xbeta), axis=1)
            return jnp.einsum('bsh,dh->bsd', jax.nn.gelu(gate, approximate=False) * h, Wo)
        return _hawk_forward(x, Wg, Wi, conv_w, conv_b, lru_Wi, lru_bi, lru_Wg, lru_bg, lam, Wo)

    def _L0_ffn_ref(x, W_r, W_k, W_v, mu_r, mu_k):
        import jax, jax.numpy as jnp
        import numpy as np
        DIM = 256

        def _reference_tuple_inner(x, W_r, W_k, W_v, mu_r, mu_k):
            B, T, C = x.shape
            x_prev = jnp.concatenate([jnp.zeros((B, 1, C), x.dtype), x[:, :-1, :]], axis=1)
            xr = mu_r * x + (1.0 - mu_r) * x_prev
            xk = mu_k * x + (1.0 - mu_k) * x_prev
            r = jax.nn.sigmoid(jnp.einsum('btc,dc->btd', xr, W_r))
            k = jnp.einsum('btc,dc->btd', xk, W_k)
            k_act = jnp.square(jax.nn.relu(k))
            out = r * jnp.einsum('btc,dc->btd', k_act, W_v)
            new_state = x[:, -1, :]
            return (out, new_state)
        return _reference_tuple_inner(x, W_r, W_k, W_v, mu_r, mu_k)[0]
    x = L0_attn_x
    xn = _layernorm(x, axis=-1)
    x = x + _L0_attn_ref(xn, L0_attn_Wg, L0_attn_Wi, L0_attn_conv_w, L0_attn_conv_b, L0_attn_lru_Wi, L0_attn_lru_bi, L0_attn_lru_Wg, L0_attn_lru_bg, L0_attn_lam, L0_attn_Wo) + _L0_ffn_ref(xn, L0_ffn_W_r, L0_ffn_W_k, L0_ffn_W_v, L0_ffn_mu_r, L0_ffn_mu_k)
    return x

_drawn_inputs = setup_inputs


def setup_inputs(seed=0):
    import zlib

    import numpy as np

    out = dict(_drawn_inputs(seed))
    spreads = {'L0_attn_lru_bi': (0.0, 0.662), 'L0_attn_lru_bg': (0.0, 0.8)}
    factors = {'L0_ffn_W_r': 3.364, 'L0_ffn_mu_r': 6.77}
    for name, (base, spread) in spreads.items():
        noise = np.random.default_rng([zlib.crc32(name.encode()), seed]).standard_normal(out[name].shape)
        drawn = base * np.exp(spread * noise) if base else spread * noise
        out[name] = jnp.asarray(drawn.astype(out[name].dtype))
    for name, factor in factors.items():
        out[name] = (out[name] * factor).astype(out[name].dtype)
    return out
```

```python
from contextlib import ExitStack

import concourse.bass as bass
from concourse import mybir

ALU = mybir.AluOpType
ACT = mybir.ActivationFunctionType
F32 = mybir.dt.float32
F32R = mybir.dt.float32r

P = 128
T = 512
TT = T // P
TAPS = 4
HALO = TAPS - 1
EPS = 1e-5

SETUP_DVE_STEPS = 21


def param_columns(D, H):
    kd, kh = D // P, H // P
    at, out = 0, {}
    for name, n in (("conv_w", kh * TAPS), ("conv_b", kh), ("bi", kh), ("bg", kh), ("lam", kh),
                    ("mu_r", kd), ("mu_k", kd)):
        out[name] = (at, n)
        at += n
    return out, at


def weight_columns(D, H):
    kd, kh = D // P, H // P
    at, out = 0, {}
    for name, k, n in (("Wi", kd, H), ("W_k", kd, D), ("Wg", kd, H), ("W_r", kd, D),
                       ("lru_Wi", kh, H), ("lru_Wg", kh, H), ("W_v", kd, D), ("Wo", kh, D)):
        out[name] = (at, k, n)
        at += k * n
    return out, at


def hawk_rwkv_block(nc: bass.Bass, x: bass.AP, weights: bass.AP, params: bass.AP, out: bass.AP, D, H):
    NTOK = x.shape[0]
    GROUPS = NTOK // T
    SEQS = GROUPS // 2
    KD, KH = D // P, H // P
    PCOL, _ = param_columns(D, H)
    WCOL, WTOTAL = weight_columns(D, H)
    assert T == 512 and KD == 2 and KH == 3 and GROUPS % 2 == 0 and WTOTAL == 4 * KH * T

    x_groups = x.rearrange("(g j p) d -> g p j d", p=P, j=TT)
    out_groups = out.rearrange("(g j p) d -> g p j d", p=P, j=TT)

    with ExitStack() as ctx:
        def sb(name, shape, dt=F32):
            return ctx.enter_context(nc.sbuf_tensor(name, shape, dt))

        def sem(name):
            return ctx.enter_context(nc.semaphore(name))

        def sems(name, n):
            return [sem(f"{name}{k}") for k in range(n)]

        psA = ctx.enter_context(nc.psum_tensor("psA", [P, KH, T], F32))
        psB = ctx.enter_context(nc.psum_tensor("psB", [P, KH, T], F32))
        psC = ctx.enter_context(nc.psum_tensor("psC", [P, KD, T], F32))
        psV = psA[:, 0:KD, :].rearrange("p a (b d) -> p (a b) d", d=D)
        psCt = psC[:, :, :].rearrange("p a (b d) -> p (a b) d", d=D)

        w_hi = sb("w_hi", [P, WTOTAL], F32R)
        w_lo = sb("w_lo", [P, WTOTAL], F32R)
        par = sb("par", [P, params.shape[1]])
        ident = sb("ident", [P, P])
        half_bi = sb("half_bi", [P, KH])
        half_bg = sb("half_bg", [P, KH])
        half_c = sb("half_c", [P, KH])
        full_c = sb("full_c", [P, KH])
        sp = sb("sp", [P, 8, KH])
        beta_bias = sb("beta_bias", [P, 1])
        minus_half = sb("minus_half", [P, TT])

        x_in = [sb(f"x_in{k}", [P, TT, D]) for k in range(2)]
        stats = sb("stats", [P, TT, 6])
        mean_var = sb("mean_var", [P, TT, 2])
        var_eps = sb("var_eps", [P, TT])
        rstd = sb("rstd", [P, TT])
        xn = sb("xn", [P, TT, D])
        tanh_r = sb("tanh_r", [P, TT, D])
        acc = [sb(f"acc{k}", [P, TT, D]) for k in range(2)]

        xt = sb("xt", [P, KD, 1 + T])
        xt_hi = sb("xt_hi", [P, KD, T], F32R)
        xt_lo = sb("xt_lo", [P, KD, T], F32R)
        xk = sb("xk", [P, KD, T])
        xk_hi = sb("xk_hi", [P, KD, T], F32R)
        xk_lo = sb("xk_lo", [P, KD, T], F32R)
        xr = sb("xr", [P, KD, T])
        xr_hi = sb("xr_hi", [P, KD, T], F32R)
        xr_lo = sb("xr_lo", [P, KD, T], F32R)
        ksq = sb("ksq", [P, KD, T])
        ksq_hi = sb("ksq_hi", [P, KD, T], F32R)
        ksq_lo = sb("ksq_lo", [P, KD, T], F32R)
        u = sb("u", [P, KH, HALO + T])
        y = sb("y", [P, KH, T])
        y_hi = sb("y_hi", [P, KH, T], F32R)
        y_lo = sb("y_lo", [P, KH, T], F32R)
        hb = [sb(f"hb{k}", [P, KH, T]) for k in range(2)]
        a2 = sb("a2", [P, KH, T])
        alpha = sb("alpha", [P, KH, T])
        z = [sb(f"z{k}", [P, KH, T]) for k in range(2)]
        z_hi = sb("z_hi", [P, KH, T], F32R)
        z_lo = sb("z_lo", [P, KH, T], F32R)
        h_last = sb("h_last", [P, KH])

        stage = [z[0], z[1], hb[0], hb[1]]
        SLAB = KH * T

        def pcol(name, k=0, n=1):
            at = PCOL[name][0]
            return par[:, at + k:at + k + n]

        def weight(tile, name, k, a, b):
            at, _, n = WCOL[name]
            return tile[:, at + k * n + a:at + k * n + b]

        w_loaded = sems("w_loaded", 4)
        p_loaded = sem("p_loaded")
        w_hi_ready = sem("w_hi_ready")
        w_lo_ready = sem("w_lo_ready")
        setup_dve = sem("setup_dve")
        setup_act = sem("setup_act")
        setup_pool = sem("setup_pool")
        x_loaded = sems("x_loaded", 2)
        out_stored = sems("out_stored", 2)
        stats_ready = sem("stats_ready")
        mean_ready = sem("mean_ready")
        vareps_ready = sem("vareps_ready")
        rstd_ready = sem("rstd_ready")
        xn_ready = sem("xn_ready")
        xt_ready = sem("xt_ready")
        xt_full = sem("xt_full")
        xt_taken = sem("xt_taken")
        xt_lo_ready = sem("xt_lo_ready")
        xt_halo = sem("xt_halo")
        diff_ready = sem("diff_ready")
        xk_ready = sems("xk_ready", KD)
        xk_hi_ready = sem("xk_hi_ready")
        xk_lo_ready = sem("xk_lo_ready")
        xr_ready = sems("xr_ready", KD)
        xr_hi_ready = sem("xr_hi_ready")
        xr_lo_ready = sem("xr_lo_ready")
        u_ready = sems("u_ready", KH)
        u_taken = sems("u_taken", KH)
        u_halo = sem("u_halo")
        conv_tap = [sems(f"conv_tap{k}_", KH) for k in range(HALO)]
        y_hi_ready = sems("y_hi_ready", KH)
        y_lo_ready = sem("y_lo_ready")
        k_ready = sem("k_ready")
        k_taken = sem("k_taken")
        ksq_ready = sem("ksq_ready")
        ksq_lo_ready = sem("ksq_lo_ready")
        gate_ready = sem("gate_ready")
        gate_taken = sem("gate_taken")
        r_ready = sem("r_ready")
        r_taken = sem("r_taken")
        ig_ready = sems("ig_ready", KH)
        ig_taken = sems("ig_taken", KH)
        rg_ready = sems("rg_ready", KH)
        rg_taken = sems("rg_taken", KH)
        alpha_ready = sem("alpha_ready")
        beta_ready = sem("beta_ready")
        iy_ready = sem("iy_ready")
        xb_ready = sem("xb_ready")
        h_ready = sem("h_ready")
        h_last_ready = sem("h_last_ready")
        z_ready = sem("z_ready")
        z_hi_ready = sem("z_hi_ready")
        z_lo_ready = sem("z_lo_ready")
        v_ready = sem("v_ready")
        v_taken = sem("v_taken")
        resid_added = sem("resid_added")
        o_ready = sem("o_ready")
        out_ready = sem("out_ready")

        def for_all_groups(eng, step):
            step(0, 0, 0, 0, False)
            step(1, 0, 1, 1, False)
            with eng.Fori(1, SEQS - 1) as seq:
                step(seq * 2, seq, 0, 2, False)
                step(seq * 2 + 1, seq, 1, 2, False)
            step(GROUPS - 2, SEQS - 1, 0, 2, False)
            step(GROUPS - 1, SEQS - 1, 1, 2, True)

        block = ctx.enter_context(nc.Block())

        @block.sync
        def _(sp_eng):
            def load_x(g, odd):
                sp_eng.dma_start(x_in[odd][:, :, :],
                                 x_groups[bass.ds(g, 1)].rearrange("g p j d -> (g p) j d")
                                 ).then_inc(x_loaded[odd], 16)

            def store(g, odd):
                sp_eng.wait_ge(out_ready, g + 1)
                sp_eng.dma_start(out_groups[bass.ds(g, 1)].rearrange("g p j d -> (g p) j d"),
                                 acc[odd][:, :, :]).then_inc(out_stored[odd], 16)

            load_x(0, 0)
            sp_eng.dma_start(par[:, :], params).then_inc(p_loaded, 16)
            for k in range(4):
                sp_eng.dma_start(stage[k][:, :, :].rearrange("p a b -> p (a b)"),
                                 weights[:, k * SLAB:(k + 1) * SLAB]).then_inc(w_loaded[k], 16)
            load_x(1, 1)

            def step(g, seq, odd, ago, last):
                if not (isinstance(g, int) and g + 2 >= GROUPS):
                    sp_eng.wait_ge(resid_added, g + 1)
                    load_x(g + 2, odd)
                if ago:
                    store(g - 1, 1 - odd)

            for_all_groups(sp_eng, step)
            store(GROUPS - 1, 1)
            for k in range(2):
                sp_eng.wait_ge(out_stored[k], 16 * SEQS)

        @block.tensor
        def _(pe):
            def product(dst, name, m, rhs_hi, rhs_lo, lo_sem, count):
                _, K, _ = WCOL[name]
                a, b = m * P, (m + 1) * P
                for k in range(K):
                    nc.tensor.matmul(dst, weight(w_hi, name, k, a, b), rhs_hi[:, k, :], start=(k == 0), stop=False)
                    nc.tensor.matmul(dst, weight(w_lo, name, k, a, b), rhs_hi[:, k, :], start=False, stop=False)
                if lo_sem is not None:
                    pe.wait_ge(lo_sem, count)
                for k in range(K):
                    mm = nc.tensor.matmul(dst, weight(w_hi, name, k, a, b), rhs_lo[:, k, :],
                                          start=False, stop=(k == K - 1))
                return mm

            def product_by_token(dst, name, lhs_hi, lhs_lo):
                _, K, n = WCOL[name]
                for j in range(TT):
                    t = slice(j * P, (j + 1) * P)
                    for k in range(K):
                        nc.tensor.matmul(dst[:, j, :], lhs_hi[:, k, t], weight(w_hi, name, k, 0, n),
                                         start=(k == 0), stop=False)
                        nc.tensor.matmul(dst[:, j, :], lhs_hi[:, k, t], weight(w_lo, name, k, 0, n),
                                         start=False, stop=False)
                    for k in range(K):
                        mm = nc.tensor.matmul(dst[:, j, :], lhs_lo[:, k, t], weight(w_hi, name, k, 0, n),
                                              start=False, stop=(k == K - 1))
                return mm

            def transpose_input(g, first):
                pe.wait_ge(xn_ready, g + 1)
                if not first:
                    pe.wait_ge(r_taken, g)
                for k in range(KD):
                    for j in range(TT):
                        mm = nc.tensor.transpose(psC[:, k, j * P:(j + 1) * P], xn[:, j, k * P:(k + 1) * P],
                                                 ident[:, :])
                mm.then_inc(xt_ready, 1)

            def project(g):
                pe.wait_ge(z_hi_ready, g + 1)
                pe.wait_ge(z_lo_ready, g + 1)
                product_by_token(psCt, "Wo", z_hi, z_lo).then_inc(o_ready, 1)

            pe.wait_ge(setup_pool, 2)
            transpose_input(0, True)
            pe.wait_ge(w_lo_ready, 4)

            def step(g, seq, odd, ago, last):
                pe.wait_ge(xt_taken, g + 1)
                if ago:
                    pe.wait_ge(v_taken, g)
                    pe.wait_ge(ig_taken[KH - 1], g)
                for c in range(KH):
                    product(psA[:, c, :], "Wi", c, xt_hi, xt_lo, xt_lo_ready if c == 0 else None, g + 1
                            ).then_inc(u_ready[c], 1)
                pe.wait_ge(xk_hi_ready, g + 1)
                if ago >= 2:
                    pe.wait_ge(out_ready, g - 1)
                for c in range(KD):
                    mm = product(psC[:, c, :], "W_k", c, xk_hi, xk_lo, xk_lo_ready if c == 0 else None, g + 1)
                mm.then_inc(k_ready, 1)
                if ago:
                    pe.wait_ge(rg_taken[KH - 1], g)
                for c in range(KH):
                    mm = product(psB[:, c, :], "Wg", c, xt_hi, xt_lo, None, 0)
                mm.then_inc(gate_ready, 1)
                pe.wait_ge(xr_hi_ready, g + 1)
                pe.wait_ge(xr_lo_ready, g + 1)
                pe.wait_ge(k_taken, g + 1)
                product_by_token(psCt, "W_r", xr_hi, xr_lo).then_inc(r_ready, 1)
                for c in range(KH):
                    pe.wait_ge(y_hi_ready[c], g + 1)
                    pe.wait_ge(u_taken[c], g + 1)
                for c in range(KH):
                    product(psA[:, c, :], "lru_Wi", c, y_hi, y_lo, y_lo_ready if c == 0 else None, g + 1
                            ).then_inc(ig_ready[c], 1)
                if not last:
                    transpose_input(g + 1, False)
                pe.wait_ge(gate_taken, g + 1)
                for c in range(KH):
                    product(psB[:, c, :], "lru_Wg", c, y_hi, y_lo, None, 0).then_inc(rg_ready[c], 1)
                pe.wait_ge(ksq_lo_ready, g + 1)
                pe.wait_ge(ig_taken[KD - 1], g + 1)
                product_by_token(psV, "W_v", ksq_hi, ksq_lo).then_inc(v_ready, 1)
                if ago:
                    if last:
                        pe.wait_ge(r_taken, g + 1)
                    else:
                        pe.wait_ge(xt_taken, g + 2)
                    project(g - 1)

            for_all_groups(pe, step)
            pe.wait_ge(out_ready, GROUPS - 1)
            project(GROUPS - 1)

        @block.scalar
        def _(act):
            va, vk, vn = WCOL["W_v"]
            vb = va + vk * vn
            for k in range(4):
                act.wait_ge(w_loaded[k], 16)
                lo, hi = k * SLAB, (k + 1) * SLAB
                raw = stage[k][:, :, :].rearrange("p a b -> p (a b)")
                parts = [(lo, hi, 1.0)]
                if lo <= va < hi:
                    parts = [(lo, va, 1.0), (va, vb, 0.5), (vb, hi, 1.0)]
                for a, b, scale in parts:
                    if b > a:
                        last = nc.scalar.activation(w_hi[:, a:b], raw[:, a - lo:b - lo], ACT.Copy, scale=scale)
                last.then_inc(w_hi_ready, 1)
                if k == 0:
                    act.wait_ge(setup_dve, 1)
                    nc.scalar.activation(sp[:, 1, :], sp[:, 0, :], ACT.Exp).then_inc(setup_act, 1)

            def take_transposed(g, first):
                act.wait_ge(xt_ready, g + 1)
                act.wait_ge(xt_halo, g + 1)
                nc.scalar.activation(xt[:, :, 1:1 + T], psC[:, :, :], ACT.Copy).then_inc(xt_full, 1)
                if not first:
                    act.wait_ge(gate_ready, g)
                nc.scalar.activation(xt_hi[:, :, :], psC[:, :, :], ACT.Copy).then_inc(xt_taken, 1)

            def make_beta(g):
                act.wait_ge(alpha_ready, g + 1)
                nc.scalar.activation(a2[:, :, :], a2[:, :, :], ACT.Sqrt, bias=beta_bias[:, 0:1],
                                     scale=-0.25 * (1 - 2.0 ** -24)).then_inc(beta_ready, 1)

            def round_z(g, odd, first):
                act.wait_ge(z_ready, g + 1)
                if not first:
                    act.wait_ge(o_ready, g)
                nc.scalar.activation(z_hi[:, :, :], z[odd][:, :, :], ACT.Copy).then_inc(z_hi_ready, 1)

            take_transposed(0, True)

            def step(g, seq, odd, ago, last):
                act.wait_ge(u_halo, g + 1)
                if ago:
                    act.wait_ge(iy_ready, g)
                for c in range(KH):
                    act.wait_ge(u_ready[c], g + 1)
                    nc.scalar.activation(u[:, c, HALO:HALO + T], psA[:, c, :], ACT.Copy)
                    nc.scalar.activation(y[:, c, :], psA[:, c, :], ACT.Identity,
                                         scale=pcol("conv_w", c * TAPS + HALO), bias=pcol("conv_b", c)
                                         ).then_inc(u_taken[c], 1)
                act.wait_ge(k_ready, g + 1)
                if ago:
                    act.wait_ge(ksq_lo_ready, g)
                nc.scalar.activation(ksq[:, :, :], psC[:, :, :], ACT.Relu).then_inc(k_taken, 1)
                act.wait_ge(k_taken, g + 1)
                if ago:
                    act.wait_ge(v_ready, g)
                nc.scalar.activation(ksq_hi[:, :, :], ksq[:, :, :], ACT.Square)
                nc.scalar.activation(ksq[:, :, :], ksq[:, :, :], ACT.Square).then_inc(ksq_ready, 1)
                if ago:
                    make_beta(g - 1)
                act.wait_ge(gate_ready, g + 1)
                if not ago:
                    act.wait_ge(w_lo_ready, 4)
                elif ago >= 2:
                    act.wait_ge(z_lo_ready, g - 1)
                nc.scalar.activation(z[odd][:, :, :], psB[:, :, :], ACT.Gelu).then_inc(gate_taken, 1)
                act.wait_ge(r_ready, g + 1)
                if ago:
                    act.wait_ge(v_taken, g)
                nc.scalar.activation(tanh_r[:, :, :], psCt, ACT.Tanh, scale=0.5).then_inc(r_taken, 1)
                if ago >= 2:
                    act.wait_ge(z_ready, g - 1)
                for c in range(KH):
                    act.wait_ge(ig_ready[c], g + 1)
                    nc.scalar.activation(hb[odd][:, c, :], psA[:, c, :], ACT.Tanh, scale=0.5,
                                         bias=half_bi[:, c:c + 1]).then_inc(ig_taken[c], 1)
                if not last:
                    take_transposed(g + 1, False)
                if ago:
                    round_z(g - 1, 1 - odd, ago < 2)
                    act.wait_ge(xb_ready, g)
                for c in range(KH):
                    act.wait_ge(rg_ready[c], g + 1)
                    nc.scalar.activation(a2[:, c, :], psB[:, c, :], ACT.Tanh, scale=0.5,
                                         bias=half_bg[:, c:c + 1]).then_inc(rg_taken[c], 1)
                if ago:
                    act.wait_ge(h_ready, g)
                for c in range(KH):
                    act.wait_ge(rg_taken[c], g + 1)
                    nc.scalar.activation(alpha[:, c, :], a2[:, c, :], ACT.Exp, scale=half_c[:, c:c + 1],
                                         bias=half_c[:, c:c + 1])
                    e = nc.scalar.activation(a2[:, c, :], a2[:, c, :], ACT.Exp, scale=full_c[:, c:c + 1],
                                             bias=full_c[:, c:c + 1])
                e.then_inc(alpha_ready, 1)

            act.wait_ge(setup_dve, SETUP_DVE_STEPS)
            act.wait_ge(setup_pool, 4)
            for_all_groups(act, step)
            make_beta(GROUPS - 1)
            round_z(GROUPS - 1, 1, False)

        @block.vector
        def _(dve):
            done = [0]

            def after(ins):
                done[0] += 1
                ins.then_inc(setup_dve, 1)
                dve.wait_ge(setup_dve, done[0])

            V = nc.vector

            def stats_of(g, seq, odd):
                dve.wait_ge(x_loaded[odd], seq * 16 + 16)
                for j in range(TT):
                    e = V.bn_stats(stats[:, j, :], x_in[odd][:, j, :])
                e.then_inc(stats_ready, 1)

            def aggregate(g, wait):
                if wait:
                    dve.wait_ge(stats_ready, g + 1)
                for j in range(TT):
                    e = V.bn_aggr(mean_var[:, j, :], stats[:, j, :])
                e.then_inc(mean_ready, 1)
                dve.wait_ge(mean_ready, g + 1)
                V.tensor_scalar(var_eps[:, :], mean_var[:, :, 1], EPS, None, ALU.add).then_inc(vareps_ready, 1)

            def normalise(g, odd, first):
                dve.wait_ge(rstd_ready, g + 1)
                if not first:
                    dve.wait_ge(xt_ready, g)
                for j in range(TT):
                    e = V.tensor_scalar(xn[:, j, :], x_in[odd][:, j, :], mean_var[:, j, 0:1], rstd[:, j:j + 1],
                                        ALU.subtract, ALU.mult)
                e.then_inc(xn_ready, 1)

            def set_xt_halo(odd):
                if odd:
                    V.tensor_copy(xt[:, :, 0:1], xt[:, :, T:T + 1]).then_inc(xt_halo, 1)
                else:
                    V.memset(xt[:, :, 0:1], 0.0).then_inc(xt_halo, 1)

            def set_u_halo(odd):
                if odd:
                    V.tensor_copy(u[:, :, 0:HALO], u[:, :, T:T + HALO]).then_inc(u_halo, 1)
                else:
                    V.memset(u[:, :, 0:HALO], 0.0).then_inc(u_halo, 1)

            def mix(g, odd, first):
                dve.wait_ge(xt_taken, g + 1)
                V.tensor_tensor(xt_lo[:, :, :], xt[:, :, 1:1 + T], xt_hi[:, :, :].bitcast(F32), ALU.subtract
                                ).then_inc(xt_lo_ready, 1)
                if not first:
                    dve.wait_ge(xr_lo_ready, g)
                V.tensor_tensor(xr[:, :, :], xt[:, :, 1:1 + T], xt[:, :, 0:T], ALU.subtract).then_inc(diff_ready, 1)
                dve.wait_ge(diff_ready, g + 1)
                if not first:
                    dve.wait_ge(xk_lo_ready, g)
                for k in range(KD):
                    V.scalar_tensor_tensor(out=xk[:, k, :], in0=xr[:, k, :], scalar=pcol("mu_k", k),
                                           in1=xt[:, k, 0:T], op0=ALU.mult, op1=ALU.add).then_inc(xk_ready[k], 1)
                for k in range(KD):
                    V.scalar_tensor_tensor(out=xr[:, k, :], in0=xr[:, k, :], scalar=pcol("mu_r", k),
                                           in1=xt[:, k, 0:T], op0=ALU.mult, op1=ALU.add).then_inc(xr_ready[k], 1)
                if not first:
                    dve.wait_ge(k_ready, g)
                    dve.wait_ge(r_ready, g)
                for k in range(KD):
                    dve.wait_ge(xk_ready[k], g + 1)
                V.tensor_copy(xk_hi[:, :, :], xk[:, :, :]).then_inc(xk_hi_ready, 1)
                for k in range(KD):
                    dve.wait_ge(xr_ready[k], g + 1)
                V.tensor_copy(xr_hi[:, :, :], xr[:, :, :]).then_inc(xr_hi_ready, 1)
                set_xt_halo(1 - odd)

            def convolve(g):
                for tap in range(HALO - 1, -1, -1):
                    for c in range(KH):
                        if tap == HALO - 1:
                            dve.wait_ge(u_taken[c], g + 1)
                        else:
                            dve.wait_ge(conv_tap[tap + 1][c], g + 1)
                        V.scalar_tensor_tensor(out=y[:, c, :], in0=u[:, c, tap:tap + T],
                                               scalar=pcol("conv_w", c * TAPS + tap), in1=y[:, c, :],
                                               op0=ALU.mult, op1=ALU.add).then_inc(conv_tap[tap][c], 1)

            def gate_input(g, odd, stats_of_group):
                if stats_of_group is not None:
                    dve.wait_ge(stats_ready, stats_of_group + 1)
                dve.wait_ge(beta_ready, g + 1)
                dve.wait_ge(iy_ready, g + 1)
                V.tensor_tensor(hb[odd][:, :, :], hb[odd][:, :, :], a2[:, :, :], ALU.mult).then_inc(xb_ready, 1)

            def recur(g, seq, odd):
                dve.wait_ge(xb_ready, g + 1)
                if odd:
                    dve.wait_ge(h_last_ready, seq + 1)
                for c in range(KH):
                    e = V.tensor_tensor_scan(hb[odd][:, c, :], alpha[:, c, :], hb[odd][:, c, :],
                                             h_last[:, c:c + 1] if odd else 0.0, ALU.mult, ALU.add)
                e.then_inc(h_ready, 1)
                dve.wait_ge(h_ready, g + 1)
                if not odd:
                    V.tensor_copy(h_last[:, :], hb[odd][:, :, T - 1]).then_inc(h_last_ready, 1)
                dve.wait_ge(gate_taken, g + 1)
                V.tensor_tensor(z[odd][:, :, :], z[odd][:, :, :], hb[odd][:, :, :], ALU.mult).then_inc(z_ready, 1)

            def finish(g, odd):
                dve.wait_ge(o_ready, g + 1)
                dve.wait_ge(resid_added, g + 1)
                V.tensor_tensor(acc[odd][:, :, :], psCt, acc[odd][:, :, :], ALU.add).then_inc(out_ready, 1)

            dve.wait_ge(p_loaded, 16)
            lam = pcol("lam", 0, KH)
            after(V.scalar_tensor_tensor(out=sp[:, 0, :], in0=lam, scalar=-1.0, in1=lam, op0=ALU.mult, op1=ALU.min))
            stats_of(0, 0, 0)
            aggregate(0, True)
            set_xt_halo(0)
            set_u_halo(0)
            normalise(0, 0, True)
            dve.wait_ge(setup_act, 1)
            after(V.tensor_scalar(sp[:, 2, :], sp[:, 1, :], 2.0, None, ALU.add))
            after(V.reciprocal(sp[:, 3, :], sp[:, 2, :]))
            after(V.tensor_tensor(sp[:, 4, :], sp[:, 1, :], sp[:, 3, :], ALU.mult))
            after(V.tensor_tensor(sp[:, 5, :], sp[:, 4, :], sp[:, 4, :], ALU.mult))
            TERMS = 9
            after(V.tensor_scalar(sp[:, 6, :], sp[:, 5, :], 1.0 / (2 * TERMS + 1), None, ALU.mult))
            for n in range(TERMS - 1, 0, -1):
                after(V.scalar_tensor_tensor(out=sp[:, 6, :], in0=sp[:, 6, :], scalar=1.0 / (2 * n + 1),
                                             in1=sp[:, 5, :], op0=ALU.add, op1=ALU.mult))
            after(V.scalar_tensor_tensor(out=sp[:, 7, :], in0=sp[:, 6, :], scalar=1.0, in1=sp[:, 4, :],
                                         op0=ALU.add, op1=ALU.mult))
            after(V.tensor_scalar(sp[:, 6, :], lam, 0.0, None, ALU.max))
            after(V.scalar_tensor_tensor(out=sp[:, 2, :], in0=sp[:, 7, :], scalar=2.0, in1=sp[:, 6, :],
                                         op0=ALU.mult, op1=ALU.add))
            after(V.tensor_scalar(half_c[:, :], sp[:, 2, :], -4.0, None, ALU.mult))
            after(V.tensor_scalar(full_c[:, :], sp[:, 2, :], -8.0, None, ALU.mult))
            after(V.tensor_scalar(half_bi[:, :], pcol("bi", 0, KH), 0.5, None, ALU.mult))
            after(V.tensor_scalar(half_bg[:, :], pcol("bg", 0, KH), 0.5, None, ALU.mult))
            assert done[0] == SETUP_DVE_STEPS
            va, vk, vn = WCOL["W_v"]
            vb = va + vk * vn
            for k in range(4):
                dve.wait_ge(w_hi_ready, k + 1)
                lo, hi = k * SLAB, (k + 1) * SLAB
                raw = stage[k][:, :, :].rearrange("p a b -> p (a b)")
                parts = [(lo, hi, 1.0)]
                if lo <= va < hi:
                    parts = [(lo, va, 1.0), (va, vb, 0.5), (vb, hi, 1.0)]
                for a, b, scale in parts:
                    if b > a:
                        e = V.scalar_tensor_tensor(out=w_lo[:, a:b], in0=raw[:, a - lo:b - lo], scalar=scale,
                                                   in1=w_hi[:, a:b].bitcast(F32), op0=ALU.mult, op1=ALU.subtract)
                e.then_inc(w_lo_ready, 1)
            mix(0, 0, True)

            def step(g, seq, odd, ago, last):
                convolve(g)
                if ago:
                    dve.wait_ge(rg_ready[KH - 1], g)
                for c in range(KH):
                    dve.wait_ge(conv_tap[0][c], g + 1)
                    V.tensor_copy(y_hi[:, c, :], y[:, c, :]).then_inc(y_hi_ready[c], 1)
                for c in range(KH):
                    dve.wait_ge(y_hi_ready[c], g + 1)
                    e = V.tensor_tensor(y_lo[:, c, :], y[:, c, :], y_hi[:, c, :].bitcast(F32), ALU.subtract)
                e.then_inc(y_lo_ready, 1)
                if not last:
                    set_u_halo(1 - odd)
                    stats_of(g + 1, seq + odd, 1 - odd)
                if ago:
                    gate_input(g - 1, 1 - odd, None if last else g + 1)
                if not last:
                    aggregate(g + 1, not ago)
                if ago:
                    recur(g - 1, seq + (odd - 1), 1 - odd)
                if not last:
                    normalise(g + 1, 1 - odd, False)
                dve.wait_ge(ig_taken[KH - 1], g + 1)
                V.scalar_tensor_tensor(out=hb[odd][:, :, :], in0=hb[odd][:, :, :], scalar=1.0, in1=y[:, :, :],
                                       op0=ALU.add, op1=ALU.mult).then_inc(iy_ready, 1)
                if not last:
                    mix(g + 1, 1 - odd, False)
                dve.wait_ge(v_ready, g + 1)
                dve.wait_ge(r_taken, g + 1)
                if ago >= 2:
                    dve.wait_ge(out_stored[odd], seq * 16)
                V.scalar_tensor_tensor(out=acc[odd][:, :, :], in0=tanh_r[:, :, :], scalar=1.0, in1=psV,
                                       op0=ALU.add, op1=ALU.mult).then_inc(v_taken, 1)
                if ago:
                    finish(g - 1, 1 - odd)

            for_all_groups(dve, step)
            gate_input(GROUPS - 1, 1, None)
            recur(GROUPS - 1, SEQS - 1, 1)
            finish(GROUPS - 1, 1)

        @block.gpsimd
        def _(pool):
            G = nc.gpsimd
            G.memset(ident[:, :], 0.0).then_inc(setup_pool, 1)
            pool.wait_ge(setup_pool, 1)
            G.affine_select(out=ident[:, :], in_=ident[:, :], compare_op=ALU.not_equal, fill=1.0, base=0,
                            pattern=[[-1, P]], channel_multiplier=1).then_inc(setup_pool, 1)
            G.memset(minus_half[:, :], -0.5).then_inc(setup_pool, 1)
            G.memset(beta_bias[:, :], 0.25 * (1 + 2.0 ** -20)).then_inc(setup_pool, 1)

            def inverse_std(g, first):
                pool.wait_ge(vareps_ready, g + 1)
                if first:
                    pool.wait_ge(setup_pool, 3)
                else:
                    pool.wait_ge(xn_ready, g)
                G.tensor_tensor(rstd[:, :], var_eps[:, :], minus_half[:, :], ALU.pow).then_inc(rstd_ready, 1)

            def split_mixes(g, first):
                pool.wait_ge(xk_hi_ready, g + 1)
                if not first:
                    pool.wait_ge(k_ready, g)
                G.tensor_tensor(xk_lo[:, :, :], xk[:, :, :], xk_hi[:, :, :].bitcast(F32), ALU.subtract
                                ).then_inc(xk_lo_ready, 1)
                pool.wait_ge(xr_hi_ready, g + 1)
                if not first:
                    pool.wait_ge(r_ready, g)
                G.tensor_tensor(xr_lo[:, :, :], xr[:, :, :], xr_hi[:, :, :].bitcast(F32), ALU.subtract
                                ).then_inc(xr_lo_ready, 1)

            def split_z(g, odd, first):
                pool.wait_ge(z_hi_ready, g + 1)
                if not first:
                    pool.wait_ge(o_ready, g)
                G.tensor_tensor(z_lo[:, :, :], z[odd][:, :, :], z_hi[:, :, :].bitcast(F32), ALU.subtract
                                ).then_inc(z_lo_ready, 1)

            inverse_std(0, True)
            split_mixes(0, True)

            def step(g, seq, odd, ago, last):
                if not last:
                    inverse_std(g + 1, False)
                pool.wait_ge(ksq_ready, g + 1)
                G.tensor_tensor(ksq_lo[:, :, :], ksq[:, :, :], ksq_hi[:, :, :].bitcast(F32), ALU.subtract
                                ).then_inc(ksq_lo_ready, 1)
                if ago:
                    split_z(g - 1, 1 - odd, ago < 2)
                if not last:
                    split_mixes(g + 1, False)
                pool.wait_ge(v_taken, g + 1)
                G.tensor_tensor(acc[odd][:, :, :], acc[odd][:, :, :], x_in[odd][:, :, :], ALU.add
                                ).then_inc(resid_added, 1)

            for_all_groups(pool, step)
            split_z(GROUPS - 1, 1, False)



def kernel(L0_attn_x, L0_attn_Wg, L0_attn_Wi, L0_attn_conv_w, L0_attn_conv_b, L0_attn_lru_Wi, L0_attn_lru_bi,
           L0_attn_lru_Wg, L0_attn_lru_bg, L0_attn_lam, L0_attn_Wo, L0_ffn_W_r, L0_ffn_W_k, L0_ffn_W_v,
           L0_ffn_mu_r, L0_ffn_mu_k):
    import numpy as np
    import concourse.bacc as bacc
    from concourse.bass_utils import run_bass_kernel_spmd

    x = np.asarray(L0_attn_x)
    B, S, D = x.shape
    H = np.asarray(L0_attn_Wg).shape[0]

    def by_input(w):
        w = np.asarray(w)
        return w.T.reshape(w.shape[1] // P, P, w.shape[0]).transpose(1, 0, 2).reshape(P, -1)

    def by_channel(v, n):
        return np.asarray(v).reshape(-1, P, n).transpose(1, 0, 2).reshape(P, -1)

    matrices = {"Wi": L0_attn_Wi, "W_k": L0_ffn_W_k, "Wg": L0_attn_Wg, "W_r": L0_ffn_W_r,
                "lru_Wi": L0_attn_lru_Wi, "lru_Wg": L0_attn_lru_Wg, "W_v": L0_ffn_W_v, "Wo": L0_attn_Wo}
    vectors = {"conv_w": (L0_attn_conv_w, TAPS), "conv_b": (L0_attn_conv_b, 1), "bi": (L0_attn_lru_bi, 1),
               "bg": (L0_attn_lru_bg, 1), "lam": (L0_attn_lam, 1), "mu_r": (L0_ffn_mu_r, 1),
               "mu_k": (L0_ffn_mu_k, 1)}
    wcol, _ = weight_columns(D, H)
    pcol, _ = param_columns(D, H)
    arrays = {
        "x": np.ascontiguousarray(x.reshape(B * S, D)),
        "weights": np.ascontiguousarray(np.concatenate([by_input(matrices[n]) for n in wcol], axis=1)),
        "params": np.ascontiguousarray(np.concatenate([by_channel(*vectors[n]) for n in pcol], axis=1)),
    }
    nc = bacc.Bacc("TRN2", target_bir_lowering=False, num_devices=1)
    args = [nc.dram_tensor(n, a.shape, mybir.dt.from_np(a.dtype), kind="ExternalInput").ap()
            for n, a in arrays.items()]
    args.append(nc.dram_tensor("out", (B * S, D), F32, kind="ExternalOutput").ap())
    hawk_rwkv_block(nc, *args, D, H)
    r = run_bass_kernel_spmd(nc, [arrays], core_ids=[0])
    return r.results[0]["out"].reshape(B, S, D)
```

```python
from contextlib import ExitStack

import concourse.bass as bass
from concourse import mybir

ALU = mybir.AluOpType
ACT = mybir.ActivationFunctionType
F32 = mybir.dt.float32
F32R = mybir.dt.float32r

P = 128
T = 512
TT = T // P
TAPS = 4
HALO = TAPS - 1
EPS = 1e-5

PARTS = 2
PT = T // PARTS
BIAS_STEPS = 3
SETUP_STEPS = 21


def param_columns(D, H):
    kd, kh = D // P, H // P
    at, out = 0, {}
    for name, n in (("conv_w", kh * TAPS), ("conv_b", kh), ("bi", kh), ("bg", kh), ("lam", kh),
                    ("mu_r", kd), ("mu_k", kd)):
        out[name] = (at, n)
        at += n
    return out, at


def weight_columns(D, H):
    kd, kh = D // P, H // P
    at, out = 0, {}
    for name, k, n in (("Wi", kd, H), ("W_k", kd, D), ("Wg", kd, H), ("W_r", kd, D),
                       ("lru_Wi", kh, H), ("lru_Wg", kh, H), ("W_v", kd, D), ("Wo", kh, D)):
        out[name] = (at, k, n)
        at += k * n
    return out, at


def hawk_rwkv_block(nc: bass.Bass, x: bass.AP, weights: bass.AP, params: bass.AP, out: bass.AP, D, H):
    NTOK = x.shape[0]
    GROUPS = NTOK // T
    SEQS = GROUPS // 2
    KD, KH = D // P, H // P
    PCOL, _ = param_columns(D, H)
    WCOL, WTOTAL = weight_columns(D, H)
    assert T == 512 and KD == 2 and KH == 3 and GROUPS % 2 == 0 and WTOTAL == 4 * KH * T

    x_groups = x.rearrange("(g j p) d -> g p j d", p=P, j=TT)
    out_groups = out.rearrange("(g j p) d -> g p j d", p=P, j=TT)

    with ExitStack() as ctx:
        def sb(name, shape, dt=F32):
            return ctx.enter_context(nc.sbuf_tensor(name, shape, dt))

        def sem(name):
            return ctx.enter_context(nc.semaphore(name))

        def sems(name, n):
            return [sem(f"{name}{k}") for k in range(n)]

        psA = ctx.enter_context(nc.psum_tensor("psA", [P, KH, T], F32))
        psB = ctx.enter_context(nc.psum_tensor("psB", [P, KH, T], F32))
        psC = ctx.enter_context(nc.psum_tensor("psC", [P, KD, T], F32))
        psV = psA[:, 0:KD, :].rearrange("p a (b d) -> p (a b) d", d=D)
        psCt = psC[:, :, :].rearrange("p a (b d) -> p (a b) d", d=D)

        w_hi = sb("w_hi", [P, WTOTAL], F32R)
        w_lo = sb("w_lo", [P, WTOTAL], F32R)
        par = sb("par", [P, params.shape[1]])
        ident = sb("ident", [P, P])
        half_bi = sb("half_bi", [P, KH])
        half_bg = sb("half_bg", [P, KH])
        half_c = sb("half_c", [P, KH])
        full_c = sb("full_c", [P, KH])
        sp = sb("sp", [P, 8, KH])
        beta_bias = sb("beta_bias", [P, 1])
        minus_half = sb("minus_half", [P, TT])

        x_in = [sb(f"x_in{k}", [P, TT, D]) for k in range(2)]
        stats = sb("stats", [P, TT, 6])
        mean_var = sb("mean_var", [P, TT, 2])
        var_eps = sb("var_eps", [P, TT])
        rstd = sb("rstd", [P, TT])
        xn = sb("xn", [P, TT, D])
        tanh_r = sb("tanh_r", [P, TT, D])
        acc = [sb(f"acc{k}", [P, TT, D]) for k in range(2)]

        xt = sb("xt", [P, KD, 1 + T])
        xt_hi = sb("xt_hi", [P, KD, T], F32R)
        xt_lo = sb("xt_lo", [P, KD, T], F32R)
        xk = sb("xk", [P, KD, T])
        xk_hi = sb("xk_hi", [P, KD, T], F32R)
        xk_lo = sb("xk_lo", [P, KD, T], F32R)
        xr = sb("xr", [P, KD, T])
        xr_hi = sb("xr_hi", [P, KD, T], F32R)
        xr_lo = sb("xr_lo", [P, KD, T], F32R)
        ksq = sb("ksq", [P, KD, T])
        ksq_hi = sb("ksq_hi", [P, KD, T], F32R)
        ksq_lo = sb("ksq_lo", [P, KD, T], F32R)
        u = sb("u", [P, KH, HALO + T])
        y = sb("y", [P, KH, T])
        y_hi = sb("y_hi", [P, KH, T], F32R)
        y_lo = sb("y_lo", [P, KH, T], F32R)
        hb = [sb(f"hb{k}", [P, KH, T]) for k in range(2)]
        a2 = sb("a2", [P, KH, T])
        alpha = sb("alpha", [P, KH, T])
        z = [sb(f"z{k}", [P, KH, T]) for k in range(2)]
        z_hi = sb("z_hi", [P, KH, T], F32R)
        z_lo = sb("z_lo", [P, KH, T], F32R)
        h_last = sb("h_last", [P, KH])

        stage = [z[0], z[1], hb[0], hb[1]]
        SLAB = KH * T

        def scaled_parts(lo, hi):
            at, k, n = WCOL["W_v"]
            parts = [(lo, at, 1.0), (at, at + k * n, 0.5), (at + k * n, hi, 1.0)] if lo <= at < hi else [(lo, hi, 1.0)]
            return [(a, b, scale) for a, b, scale in parts if b > a]

        def pcol(name, k=0, n=1):
            at = PCOL[name][0]
            return par[:, at + k:at + k + n]

        def weight(tile, name, k, a, b):
            at, _, n = WCOL[name]
            return tile[:, at + k * n + a:at + k * n + b]

        w_loaded = sems("w_loaded", 4)
        p_loaded = sem("p_loaded")
        w_hi_ready = sem("w_hi_ready")
        w_lo_ready = sems("w_lo_ready", 4)
        setup_dve = sem("setup_dve")
        setup_act = sem("setup_act")
        setup_pool = sem("setup_pool")
        x_loaded = sems("x_loaded", 2)
        out_stored = sems("out_stored", 2)
        stats_ready = sem("stats_ready")
        mean_ready = sem("mean_ready")
        vareps_ready = sem("vareps_ready")
        rstd_ready = sem("rstd_ready")
        xn_ready = sem("xn_ready")
        xt_ready = sem("xt_ready")
        xt_hi_ready = sem("xt_hi_ready")
        xt_taken = sem("xt_taken")
        xt_lo_ready = sem("xt_lo_ready")
        xt_halo = sem("xt_halo")
        diff_ready = sem("diff_ready")
        xk_ready = sems("xk_ready", KD)
        xk_hi_ready = sem("xk_hi_ready")
        xk_lo_ready = sem("xk_lo_ready")
        xr_ready = sems("xr_ready", KD)
        xr_hi_ready = sem("xr_hi_ready")
        xr_lo_ready = sem("xr_lo_ready")
        u_ready = sems("u_ready", KH)
        u_taken = sems("u_taken", KH)
        u_halo = sem("u_halo")
        conv_tap = [sems(f"conv_tap{k}_", KH) for k in range(HALO)]
        y_hi_ready = sems("y_hi_ready", KH)
        y_lo_ready = sem("y_lo_ready")
        k_ready = sem("k_ready")
        k_taken = sem("k_taken")
        ksq_ready = sem("ksq_ready")
        ksq_lo_ready = sem("ksq_lo_ready")
        gate_ready = sem("gate_ready")
        gate_taken = sem("gate_taken")
        r_ready = sem("r_ready")
        r_taken = sem("r_taken")
        ig_ready = sems("ig_ready", KH)
        ig_taken = sems("ig_taken", KH)
        rg_ready = sems("rg_ready", KH)
        rg_taken = sems("rg_taken", KH)
        alpha_ready = sem("alpha_ready")
        beta_ready = sem("beta_ready")
        iy_ready = sem("iy_ready")
        xb_ready = sem("xb_ready")
        h_ready = sem("h_ready")
        h_last_ready = sem("h_last_ready")
        z_ready = sem("z_ready")
        z_hi_ready = sem("z_hi_ready")
        z_lo_ready = sem("z_lo_ready")
        v_ready = sem("v_ready")
        v_taken = sem("v_taken")
        resid_added = sem("resid_added")
        o_ready = sem("o_ready")
        out_ready = sem("out_ready")
        end_beta = sem("end_beta")
        end_xb = sem("end_xb")
        end_h = sem("end_h")
        end_z = sem("end_z")
        end_z_hi = sem("end_z_hi")
        end_z_lo = sem("end_z_lo")
        end_o = sem("end_o")
        end_out = sem("end_out")
        end_stored = sem("end_stored")

        def for_all_groups(eng, step):
            step(0, 0, 0, 0, False)
            step(1, 0, 1, 1, False)
            with eng.Fori(1, SEQS - 1) as seq:
                step(seq * 2, seq, 0, 2, False)
                step(seq * 2 + 1, seq, 1, 2, False)
            step(GROUPS - 2, SEQS - 1, 0, 2, False)
            step(GROUPS - 1, SEQS - 1, 1, 2, True)

        block = ctx.enter_context(nc.Block())

        @block.sync
        def _(sp_eng):
            def load_x(g, odd):
                sp_eng.dma_start(x_in[odd][:, :, :],
                                 x_groups[bass.ds(g, 1)].rearrange("g p j d -> (g p) j d")
                                 ).then_inc(x_loaded[odd], 16)

            def store(g, odd):
                sp_eng.wait_ge(out_ready, g + 1)
                sp_eng.dma_start(out_groups[bass.ds(g, 1)].rearrange("g p j d -> (g p) j d"),
                                 acc[odd][:, :, :]).then_inc(out_stored[odd], 16)

            load_x(0, 0)
            sp_eng.dma_start(par[:, :], params).then_inc(p_loaded, 16)
            for k in range(4):
                sp_eng.dma_start(stage[k][:, :, :].rearrange("p a b -> p (a b)"),
                                 weights[:, k * SLAB:(k + 1) * SLAB]).then_inc(w_loaded[k], 16)
            load_x(1, 1)

            def step(g, seq, odd, ago, last):
                if not (isinstance(g, int) and g + 2 >= GROUPS):
                    sp_eng.wait_ge(resid_added, g + 1)
                    load_x(g + 2, odd)
                if ago:
                    store(g - 1, 1 - odd)

            for_all_groups(sp_eng, step)
            for n in range(PARTS):
                sp_eng.wait_ge(end_out, n + 1)
                tiles = slice(n * TT // PARTS, (n + 1) * TT // PARTS)
                sp_eng.dma_start(out_groups[GROUPS - 1][:, tiles, :], acc[1][:, tiles, :]).then_inc(end_stored, 16)
            sp_eng.wait_ge(out_stored[0], 16 * SEQS)
            sp_eng.wait_ge(out_stored[1], 16 * (SEQS - 1))
            sp_eng.wait_ge(end_stored, 16 * PARTS)

        @block.tensor
        def _(pe):
            def product(dst, name, m, rhs_hi, rhs_lo, lo_sem, count):
                _, K, _ = WCOL[name]
                a, b = m * P, (m + 1) * P
                for k in range(K):
                    nc.tensor.matmul(dst, weight(w_hi, name, k, a, b), rhs_hi[:, k, :], start=(k == 0), stop=False)
                    nc.tensor.matmul(dst, weight(w_lo, name, k, a, b), rhs_hi[:, k, :], start=False, stop=False)
                if lo_sem is not None:
                    pe.wait_ge(lo_sem, count)
                for k in range(K):
                    mm = nc.tensor.matmul(dst, weight(w_hi, name, k, a, b), rhs_lo[:, k, :],
                                          start=False, stop=(k == K - 1))
                return mm

            def product_by_token(dst, name, lhs_hi, lhs_lo, tiles=range(TT)):
                _, K, n = WCOL[name]
                for j in tiles:
                    t = slice(j * P, (j + 1) * P)
                    for k in range(K):
                        nc.tensor.matmul(dst[:, j, :], lhs_hi[:, k, t], weight(w_hi, name, k, 0, n),
                                         start=(k == 0), stop=False)
                        nc.tensor.matmul(dst[:, j, :], lhs_hi[:, k, t], weight(w_lo, name, k, 0, n),
                                         start=False, stop=False)
                    for k in range(K):
                        mm = nc.tensor.matmul(dst[:, j, :], lhs_lo[:, k, t], weight(w_hi, name, k, 0, n),
                                              start=False, stop=(k == K - 1))
                return mm

            def transpose_input(g, first):
                pe.wait_ge(xn_ready, g + 1)
                if not first:
                    pe.wait_ge(r_taken, g)
                for k in range(KD):
                    for j in range(TT):
                        mm = nc.tensor.transpose(psC[:, k, j * P:(j + 1) * P], xn[:, j, k * P:(k + 1) * P],
                                                 ident[:, :])
                mm.then_inc(xt_ready, 1)

            def project(g):
                pe.wait_ge(z_hi_ready, g + 1)
                pe.wait_ge(z_lo_ready, g + 1)
                product_by_token(psCt, "Wo", z_hi, z_lo).then_inc(o_ready, 1)

            pe.wait_ge(setup_pool, 2)
            transpose_input(0, True)

            def step(g, seq, odd, ago, last):
                if not ago:
                    pe.wait_ge(w_lo_ready[0], 1)
                pe.wait_ge(xt_hi_ready, g + 1)
                if ago:
                    pe.wait_ge(v_taken, g)
                    pe.wait_ge(ig_taken[KH - 1], g)
                for c in range(KH):
                    product(psA[:, c, :], "Wi", c, xt_hi, xt_lo, xt_lo_ready if c == 0 else None, g + 1
                            ).then_inc(u_ready[c], 1)
                pe.wait_ge(xk_hi_ready, g + 1)
                if ago >= 2:
                    pe.wait_ge(out_ready, g - 1)
                for c in range(KD):
                    mm = product(psC[:, c, :], "W_k", c, xk_hi, xk_lo, xk_lo_ready if c == 0 else None, g + 1)
                mm.then_inc(k_ready, 1)
                if not ago:
                    pe.wait_ge(w_lo_ready[1], 1)
                if ago:
                    pe.wait_ge(rg_taken[KH - 1], g)
                for c in range(KH):
                    mm = product(psB[:, c, :], "Wg", c, xt_hi, xt_lo, None, 0)
                mm.then_inc(gate_ready, 1)
                pe.wait_ge(xr_hi_ready, g + 1)
                pe.wait_ge(xr_lo_ready, g + 1)
                pe.wait_ge(k_taken, g + 1)
                product_by_token(psCt, "W_r", xr_hi, xr_lo).then_inc(r_ready, 1)
                if not ago:
                    pe.wait_ge(w_lo_ready[2], 1)
                for c in range(KH):
                    pe.wait_ge(y_hi_ready[c], g + 1)
                    pe.wait_ge(u_taken[c], g + 1)
                for c in range(KH):
                    product(psA[:, c, :], "lru_Wi", c, y_hi, y_lo, y_lo_ready if c == 0 else None, g + 1
                            ).then_inc(ig_ready[c], 1)
                if not last:
                    transpose_input(g + 1, False)
                if not ago:
                    pe.wait_ge(w_lo_ready[3], 1)
                pe.wait_ge(gate_taken, g + 1)
                for c in range(KH):
                    product(psB[:, c, :], "lru_Wg", c, y_hi, y_lo, None, 0).then_inc(rg_ready[c], 1)
                pe.wait_ge(ksq_lo_ready, g + 1)
                pe.wait_ge(ig_taken[KD - 1], g + 1)
                product_by_token(psV, "W_v", ksq_hi, ksq_lo).then_inc(v_ready, 1)
                if ago:
                    if last:
                        pe.wait_ge(r_taken, g + 1)
                    else:
                        pe.wait_ge(xt_taken, g + 2)
                    project(g - 1)

            for_all_groups(pe, step)
            pe.wait_ge(out_ready, GROUPS - 1)
            for n in range(PARTS):
                pe.wait_ge(end_z_hi, n + 1)
                pe.wait_ge(end_z_lo, n + 1)
                product_by_token(psCt, "Wo", z_hi, z_lo, range(n * TT // PARTS, (n + 1) * TT // PARTS)
                                 ).then_inc(end_o, 1)

        @block.scalar
        def _(act):
            def round_weights(k):
                act.wait_ge(w_loaded[k], 16)
                lo, hi = k * SLAB, (k + 1) * SLAB
                raw = stage[k][:, :, :].rearrange("p a b -> p (a b)")
                for a, b, scale in scaled_parts(lo, hi):
                    last = nc.scalar.activation(w_hi[:, a:b], raw[:, a - lo:b - lo], ACT.Copy, scale=scale)
                last.then_inc(w_hi_ready, 1)
                if k == 0:
                    act.wait_ge(setup_dve, 1)
                    nc.scalar.activation(sp[:, 1, :], sp[:, 0, :], ACT.Exp).then_inc(setup_act, 1)

            for k in range(2):
                round_weights(k)

            def take_transposed(g, first):
                act.wait_ge(xt_ready, g + 1)
                act.wait_ge(xt_halo, g + 1)
                if not first:
                    act.wait_ge(gate_ready, g)
                nc.scalar.activation(xt_hi[:, :, :], psC[:, :, :], ACT.Copy).then_inc(xt_hi_ready, 1)
                nc.scalar.activation(xt[:, :, 1:1 + T], psC[:, :, :], ACT.Copy).then_inc(xt_taken, 1)

            def make_beta(g):
                act.wait_ge(alpha_ready, g + 1)
                nc.scalar.activation(a2[:, :, :], a2[:, :, :], ACT.Sqrt, bias=beta_bias[:, 0:1],
                                     scale=-0.25 * (1 - 2.0 ** -24)).then_inc(beta_ready, 1)

            def round_z(g, odd, first):
                act.wait_ge(z_ready, g + 1)
                if not first:
                    act.wait_ge(o_ready, g)
                nc.scalar.activation(z_hi[:, :, :], z[odd][:, :, :], ACT.Copy).then_inc(z_hi_ready, 1)

            take_transposed(0, True)
            for k in range(2, 4):
                round_weights(k)

            def step(g, seq, odd, ago, last):
                act.wait_ge(u_halo, g + 1)
                if ago:
                    act.wait_ge(iy_ready, g)
                for c in range(KH):
                    act.wait_ge(u_ready[c], g + 1)
                    nc.scalar.activation(u[:, c, HALO:HALO + T], psA[:, c, :], ACT.Copy)
                    nc.scalar.activation(y[:, c, :], psA[:, c, :], ACT.Identity,
                                         scale=pcol("conv_w", c * TAPS + HALO), bias=pcol("conv_b", c)
                                         ).then_inc(u_taken[c], 1)
                act.wait_ge(k_ready, g + 1)
                if ago:
                    act.wait_ge(ksq_lo_ready, g)
                nc.scalar.activation(ksq[:, :, :], psC[:, :, :], ACT.Relu).then_inc(k_taken, 1)
                act.wait_ge(k_taken, g + 1)
                if ago:
                    act.wait_ge(v_ready, g)
                nc.scalar.activation(ksq_hi[:, :, :], ksq[:, :, :], ACT.Square)
                nc.scalar.activation(ksq[:, :, :], ksq[:, :, :], ACT.Square).then_inc(ksq_ready, 1)
                act.wait_ge(gate_ready, g + 1)
                if not ago:
                    for k in range(4):
                        act.wait_ge(w_lo_ready[k], 1)
                elif ago >= 2:
                    act.wait_ge(z_lo_ready, g - 1)
                nc.scalar.activation(z[odd][:, :, :], psB[:, :, :], ACT.Gelu).then_inc(gate_taken, 1)
                act.wait_ge(r_ready, g + 1)
                if ago:
                    act.wait_ge(v_taken, g)
                nc.scalar.activation(tanh_r[:, :, :], psCt, ACT.Tanh, scale=0.5).then_inc(r_taken, 1)
                if ago >= 2:
                    act.wait_ge(z_ready, g - 1)
                for c in range(KH):
                    act.wait_ge(ig_ready[c], g + 1)
                    nc.scalar.activation(hb[odd][:, c, :], psA[:, c, :], ACT.Tanh, scale=0.5,
                                         bias=half_bi[:, c:c + 1]).then_inc(ig_taken[c], 1)
                if not last:
                    take_transposed(g + 1, False)
                if ago:
                    round_z(g - 1, 1 - odd, ago < 2)
                    act.wait_ge(h_ready, g)
                if not ago:
                    act.wait_ge(setup_dve, SETUP_STEPS)
                for c in range(KH):
                    act.wait_ge(rg_ready[c], g + 1)
                    nc.scalar.activation(a2[:, c, :], psB[:, c, :], ACT.Tanh, scale=0.5,
                                         bias=half_bg[:, c:c + 1]).then_inc(rg_taken[c], 1)
                    act.wait_ge(rg_taken[c], g + 1)
                    nc.scalar.activation(alpha[:, c, :], a2[:, c, :], ACT.Exp, scale=half_c[:, c:c + 1],
                                         bias=half_c[:, c:c + 1])
                    e = nc.scalar.activation(a2[:, c, :], a2[:, c, :], ACT.Exp, scale=full_c[:, c:c + 1],
                                             bias=full_c[:, c:c + 1])
                e.then_inc(alpha_ready, 1)
                if not last:
                    make_beta(g)

            act.wait_ge(setup_dve, BIAS_STEPS)
            act.wait_ge(setup_pool, 4)
            for_all_groups(act, step)
            act.wait_ge(alpha_ready, GROUPS)
            for n in range(PARTS):
                t = slice(n * PT, (n + 1) * PT)
                nc.scalar.activation(a2[:, :, t], a2[:, :, t], ACT.Sqrt, bias=beta_bias[:, 0:1],
                                     scale=-0.25 * (1 - 2.0 ** -24)).then_inc(end_beta, 1)
            act.wait_ge(o_ready, GROUPS - 1)
            for n in range(PARTS):
                t = slice(n * PT, (n + 1) * PT)
                act.wait_ge(end_z, n + 1)
                nc.scalar.activation(z_hi[:, :, t], z[1][:, :, t], ACT.Copy).then_inc(end_z_hi, 1)

        @block.vector
        def _(dve):
            done = [0]

            def after(ins):
                done[0] += 1
                ins.then_inc(setup_dve, 1)
                dve.wait_ge(setup_dve, done[0])

            V = nc.vector

            def stats_of(g, seq, odd):
                dve.wait_ge(x_loaded[odd], seq * 16 + 16)
                for j in range(TT):
                    e = V.bn_stats(stats[:, j, :], x_in[odd][:, j, :])
                e.then_inc(stats_ready, 1)

            def aggregate(g):
                for j in range(TT):
                    e = V.bn_aggr(mean_var[:, j, :], stats[:, j, :])
                e.then_inc(mean_ready, 1)
                dve.wait_ge(mean_ready, g + 1)
                V.tensor_scalar(var_eps[:, :], mean_var[:, :, 1], EPS, None, ALU.add).then_inc(vareps_ready, 1)

            def normalise(g, odd, first):
                dve.wait_ge(rstd_ready, g + 1)
                if not first:
                    dve.wait_ge(xt_ready, g)
                for j in range(TT):
                    e = V.tensor_scalar(xn[:, j, :], x_in[odd][:, j, :], mean_var[:, j, 0:1], rstd[:, j:j + 1],
                                        ALU.subtract, ALU.mult)
                e.then_inc(xn_ready, 1)

            def set_xt_halo(odd):
                if odd:
                    V.tensor_copy(xt[:, :, 0:1], xt[:, :, T:T + 1]).then_inc(xt_halo, 1)
                else:
                    V.memset(xt[:, :, 0:1], 0.0).then_inc(xt_halo, 1)

            def set_u_halo(odd):
                if odd:
                    V.tensor_copy(u[:, :, 0:HALO], u[:, :, T:T + HALO]).then_inc(u_halo, 1)
                else:
                    V.memset(u[:, :, 0:HALO], 0.0).then_inc(u_halo, 1)

            def mix(g, odd, first):
                dve.wait_ge(xt_taken, g + 1)
                V.tensor_tensor(xt_lo[:, :, :], xt[:, :, 1:1 + T], xt_hi[:, :, :].bitcast(F32), ALU.subtract
                                ).then_inc(xt_lo_ready, 1)
                if not first:
                    dve.wait_ge(xr_lo_ready, g)
                V.tensor_tensor(xr[:, :, :], xt[:, :, 1:1 + T], xt[:, :, 0:T], ALU.subtract).then_inc(diff_ready, 1)
                dve.wait_ge(diff_ready, g + 1)
                if not first:
                    dve.wait_ge(xk_lo_ready, g)
                for k in range(KD):
                    V.scalar_tensor_tensor(out=xk[:, k, :], in0=xr[:, k, :], scalar=pcol("mu_k", k),
                                           in1=xt[:, k, 0:T], op0=ALU.mult, op1=ALU.add).then_inc(xk_ready[k], 1)
                for k in range(KD):
                    V.scalar_tensor_tensor(out=xr[:, k, :], in0=xr[:, k, :], scalar=pcol("mu_r", k),
                                           in1=xt[:, k, 0:T], op0=ALU.mult, op1=ALU.add).then_inc(xr_ready[k], 1)
                if not first:
                    dve.wait_ge(k_ready, g)
                    dve.wait_ge(r_ready, g)
                for k in range(KD):
                    dve.wait_ge(xk_ready[k], g + 1)
                V.tensor_copy(xk_hi[:, :, :], xk[:, :, :]).then_inc(xk_hi_ready, 1)
                for k in range(KD):
                    dve.wait_ge(xr_ready[k], g + 1)
                V.tensor_copy(xr_hi[:, :, :], xr[:, :, :]).then_inc(xr_hi_ready, 1)
                set_xt_halo(1 - odd)

            def convolve_tap(g, tap):
                for c in range(KH):
                    if tap == HALO - 1:
                        dve.wait_ge(u_taken[c], g + 1)
                    else:
                        dve.wait_ge(conv_tap[tap + 1][c], g + 1)
                    V.scalar_tensor_tensor(out=y[:, c, :], in0=u[:, c, tap:tap + T],
                                           scalar=pcol("conv_w", c * TAPS + tap), in1=y[:, c, :],
                                           op0=ALU.mult, op1=ALU.add).then_inc(conv_tap[tap][c], 1)

            def gate_input(g, odd):
                dve.wait_ge(beta_ready, g + 1)
                dve.wait_ge(iy_ready, g + 1)
                V.tensor_tensor(hb[odd][:, :, :], hb[odd][:, :, :], a2[:, :, :], ALU.mult).then_inc(xb_ready, 1)

            def recur(g, seq, odd):
                dve.wait_ge(xb_ready, g + 1)
                if odd:
                    dve.wait_ge(h_last_ready, seq + 1)
                for c in range(KH):
                    e = V.tensor_tensor_scan(hb[odd][:, c, :], alpha[:, c, :], hb[odd][:, c, :],
                                             h_last[:, c:c + 1] if odd else 0.0, ALU.mult, ALU.add)
                e.then_inc(h_ready, 1)
                dve.wait_ge(h_ready, g + 1)
                if not odd:
                    V.tensor_copy(h_last[:, :], hb[odd][:, :, T - 1]).then_inc(h_last_ready, 1)
                dve.wait_ge(gate_taken, g + 1)
                V.tensor_tensor(z[odd][:, :, :], z[odd][:, :, :], hb[odd][:, :, :], ALU.mult).then_inc(z_ready, 1)

            def finish(g, odd):
                dve.wait_ge(o_ready, g + 1)
                dve.wait_ge(resid_added, g + 1)
                V.tensor_tensor(acc[odd][:, :, :], psCt, acc[odd][:, :, :], ALU.add).then_inc(out_ready, 1)

            def derive_decay():
                dve.wait_ge(setup_act, 1)
                after(V.tensor_scalar(sp[:, 2, :], sp[:, 1, :], 2.0, None, ALU.add))
                after(V.reciprocal(sp[:, 3, :], sp[:, 2, :]))
                after(V.tensor_tensor(sp[:, 4, :], sp[:, 1, :], sp[:, 3, :], ALU.mult))
                after(V.tensor_tensor(sp[:, 5, :], sp[:, 4, :], sp[:, 4, :], ALU.mult))
                TERMS = 9
                after(V.tensor_scalar(sp[:, 6, :], sp[:, 5, :], 1.0 / (2 * TERMS + 1), None, ALU.mult))
                for n in range(TERMS - 1, 0, -1):
                    after(V.scalar_tensor_tensor(out=sp[:, 6, :], in0=sp[:, 6, :], scalar=1.0 / (2 * n + 1),
                                                 in1=sp[:, 5, :], op0=ALU.add, op1=ALU.mult))
                after(V.scalar_tensor_tensor(out=sp[:, 7, :], in0=sp[:, 6, :], scalar=1.0, in1=sp[:, 4, :],
                                             op0=ALU.add, op1=ALU.mult))
                after(V.tensor_scalar(sp[:, 6, :], lam, 0.0, None, ALU.max))
                after(V.scalar_tensor_tensor(out=sp[:, 2, :], in0=sp[:, 7, :], scalar=2.0, in1=sp[:, 6, :],
                                             op0=ALU.mult, op1=ALU.add))
                after(V.tensor_scalar(half_c[:, :], sp[:, 2, :], -4.0, None, ALU.mult))
                after(V.tensor_scalar(full_c[:, :], sp[:, 2, :], -8.0, None, ALU.mult))
                assert done[0] == SETUP_STEPS

            def split_weights(k):
                dve.wait_ge(w_hi_ready, k + 1)
                lo, hi = k * SLAB, (k + 1) * SLAB
                raw = stage[k][:, :, :].rearrange("p a b -> p (a b)")
                for a, b, scale in scaled_parts(lo, hi):
                    e = V.scalar_tensor_tensor(out=w_lo[:, a:b], in0=raw[:, a - lo:b - lo], scalar=scale,
                                               in1=w_hi[:, a:b].bitcast(F32), op0=ALU.mult, op1=ALU.subtract)
                e.then_inc(w_lo_ready[k], 1)

            stats_of(0, 0, 0)
            dve.wait_ge(stats_ready, 1)
            aggregate(0)
            set_xt_halo(0)
            set_u_halo(0)
            dve.wait_ge(p_loaded, 16)
            lam = pcol("lam", 0, KH)
            after(V.scalar_tensor_tensor(out=sp[:, 0, :], in0=lam, scalar=-1.0, in1=lam, op0=ALU.mult, op1=ALU.min))
            after(V.tensor_scalar(half_bi[:, :], pcol("bi", 0, KH), 0.5, None, ALU.mult))
            after(V.tensor_scalar(half_bg[:, :], pcol("bg", 0, KH), 0.5, None, ALU.mult))
            assert done[0] == BIAS_STEPS
            normalise(0, 0, True)
            split_weights(0)
            mix(0, 0, True)
            split_weights(3)

            def step(g, seq, odd, ago, last):
                convolve_tap(g, 2)
                if not last:
                    stats_of(g + 1, seq + odd, 1 - odd)
                convolve_tap(g, 1)
                convolve_tap(g, 0)
                if ago:
                    dve.wait_ge(rg_ready[KH - 1], g)
                for c in range(KH):
                    dve.wait_ge(conv_tap[0][c], g + 1)
                    V.tensor_copy(y_hi[:, c, :], y[:, c, :]).then_inc(y_hi_ready[c], 1)
                if not last:
                    dve.wait_ge(stats_ready, g + 2)
                for c in range(KH):
                    dve.wait_ge(y_hi_ready[c], g + 1)
                    e = V.tensor_tensor(y_lo[:, c, :], y[:, c, :], y_hi[:, c, :].bitcast(F32), ALU.subtract)
                e.then_inc(y_lo_ready, 1)
                if not last:
                    set_u_halo(1 - odd)
                    aggregate(g + 1)
                if ago:
                    gate_input(g - 1, 1 - odd)
                if not last:
                    normalise(g + 1, 1 - odd, False)
                if ago:
                    recur(g - 1, seq + (odd - 1), 1 - odd)
                else:
                    derive_decay()
                dve.wait_ge(ig_taken[KH - 1], g + 1)
                V.scalar_tensor_tensor(out=hb[odd][:, :, :], in0=hb[odd][:, :, :], scalar=1.0, in1=y[:, :, :],
                                       op0=ALU.add, op1=ALU.mult).then_inc(iy_ready, 1)
                if not last:
                    mix(g + 1, 1 - odd, False)
                dve.wait_ge(v_ready, g + 1)
                dve.wait_ge(r_taken, g + 1)
                if ago >= 2:
                    dve.wait_ge(out_stored[odd], seq * 16)
                V.scalar_tensor_tensor(out=acc[odd][:, :, :], in0=tanh_r[:, :, :], scalar=1.0, in1=psV,
                                       op0=ALU.add, op1=ALU.mult).then_inc(v_taken, 1)
                if ago and not last:
                    finish(g - 1, 1 - odd)

            for_all_groups(dve, step)
            dve.wait_ge(h_last_ready, SEQS)
            dve.wait_ge(iy_ready, GROUPS)
            dve.wait_ge(gate_taken, GROUPS)
            for n in range(PARTS):
                t = slice(n * PT, (n + 1) * PT)
                dve.wait_ge(end_beta, n + 1)
                V.tensor_tensor(hb[1][:, :, t], hb[1][:, :, t], a2[:, :, t], ALU.mult).then_inc(end_xb, 1)
                dve.wait_ge(end_xb, n + 1)
                for c in range(KH):
                    before = hb[1][:, c, n * PT - 1:n * PT] if n else h_last[:, c:c + 1]
                    e = V.tensor_tensor_scan(hb[1][:, c, t], alpha[:, c, t], hb[1][:, c, t], before,
                                             ALU.mult, ALU.add)
                e.then_inc(end_h, 1)
                dve.wait_ge(end_h, n + 1)
                V.tensor_tensor(z[1][:, :, t], z[1][:, :, t], hb[1][:, :, t], ALU.mult).then_inc(end_z, 1)
                if n == 0:
                    finish(GROUPS - 2, 0)
            dve.wait_ge(resid_added, GROUPS)
            for n in range(PARTS):
                tiles = slice(n * TT // PARTS, (n + 1) * TT // PARTS)
                dve.wait_ge(end_o, n + 1)
                V.tensor_tensor(acc[1][:, tiles, :], psCt[:, tiles, :], acc[1][:, tiles, :], ALU.add
                                ).then_inc(end_out, 1)

        @block.gpsimd
        def _(pool):
            G = nc.gpsimd
            G.memset(ident[:, :], 0.0).then_inc(setup_pool, 1)
            pool.wait_ge(setup_pool, 1)
            G.affine_select(out=ident[:, :], in_=ident[:, :], compare_op=ALU.not_equal, fill=1.0, base=0,
                            pattern=[[-1, P]], channel_multiplier=1).then_inc(setup_pool, 1)
            G.memset(minus_half[:, :], -0.5).then_inc(setup_pool, 1)
            G.memset(beta_bias[:, :], 0.25 * (1 + 2.0 ** -20)).then_inc(setup_pool, 1)

            def inverse_std(g, first):
                pool.wait_ge(vareps_ready, g + 1)
                if first:
                    pool.wait_ge(setup_pool, 3)
                else:
                    pool.wait_ge(xn_ready, g)
                G.tensor_tensor(rstd[:, :], var_eps[:, :], minus_half[:, :], ALU.pow).then_inc(rstd_ready, 1)

            def split_xk(g, first):
                pool.wait_ge(xk_hi_ready, g + 1)
                if not first:
                    pool.wait_ge(k_ready, g)
                G.tensor_tensor(xk_lo[:, :, :], xk[:, :, :], xk_hi[:, :, :].bitcast(F32), ALU.subtract
                                ).then_inc(xk_lo_ready, 1)

            def split_xr(g, first):
                pool.wait_ge(xr_hi_ready, g + 1)
                if not first:
                    pool.wait_ge(r_ready, g)
                G.tensor_tensor(xr_lo[:, :, :], xr[:, :, :], xr_hi[:, :, :].bitcast(F32), ALU.subtract
                                ).then_inc(xr_lo_ready, 1)

            def split_z(g, odd, first):
                pool.wait_ge(z_hi_ready, g + 1)
                if not first:
                    pool.wait_ge(o_ready, g)
                G.tensor_tensor(z_lo[:, :, :], z[odd][:, :, :], z_hi[:, :, :].bitcast(F32), ALU.subtract
                                ).then_inc(z_lo_ready, 1)

            inverse_std(0, True)
            for k in (1, 2):
                pool.wait_ge(w_hi_ready, k + 1)
                G.tensor_tensor(w_lo[:, k * SLAB:(k + 1) * SLAB], stage[k][:, :, :].rearrange("p a b -> p (a b)"),
                                w_hi[:, k * SLAB:(k + 1) * SLAB].bitcast(F32), ALU.subtract
                                ).then_inc(w_lo_ready[k], 1)
            split_xk(0, True)
            split_xr(0, True)

            def step(g, seq, odd, ago, last):
                if not last:
                    inverse_std(g + 1, False)
                pool.wait_ge(ksq_ready, g + 1)
                G.tensor_tensor(ksq_lo[:, :, :], ksq[:, :, :], ksq_hi[:, :, :].bitcast(F32), ALU.subtract
                                ).then_inc(ksq_lo_ready, 1)
                if ago:
                    split_z(g - 1, 1 - odd, ago < 2)
                if not last:
                    split_xk(g + 1, False)
                pool.wait_ge(v_taken, g + 1)
                G.tensor_tensor(acc[odd][:, :, :], acc[odd][:, :, :], x_in[odd][:, :, :], ALU.add
                                ).then_inc(resid_added, 1)
                if not last:
                    split_xr(g + 1, False)

            for_all_groups(pool, step)
            pool.wait_ge(o_ready, GROUPS - 1)
            for n in range(PARTS):
                t = slice(n * PT, (n + 1) * PT)
                pool.wait_ge(end_z_hi, n + 1)
                G.tensor_tensor(z_lo[:, :, t], z[1][:, :, t], z_hi[:, :, t].bitcast(F32), ALU.subtract
                                ).then_inc(end_z_lo, 1)



def kernel(L0_attn_x, L0_attn_Wg, L0_attn_Wi, L0_attn_conv_w, L0_attn_conv_b, L0_attn_lru_Wi, L0_attn_lru_bi,
           L0_attn_lru_Wg, L0_attn_lru_bg, L0_attn_lam, L0_attn_Wo, L0_ffn_W_r, L0_ffn_W_k, L0_ffn_W_v,
           L0_ffn_mu_r, L0_ffn_mu_k):
    import numpy as np
    import concourse.bacc as bacc
    from concourse.bass_utils import run_bass_kernel_spmd

    x = np.asarray(L0_attn_x)
    B, S, D = x.shape
    H = np.asarray(L0_attn_Wg).shape[0]

    def by_input(w):
        w = np.asarray(w)
        return w.T.reshape(w.shape[1] // P, P, w.shape[0]).transpose(1, 0, 2).reshape(P, -1)

    def by_channel(v, n):
        return np.asarray(v).reshape(-1, P, n).transpose(1, 0, 2).reshape(P, -1)

    matrices = {"Wi": L0_attn_Wi, "W_k": L0_ffn_W_k, "Wg": L0_attn_Wg, "W_r": L0_ffn_W_r,
                "lru_Wi": L0_attn_lru_Wi, "lru_Wg": L0_attn_lru_Wg, "W_v": L0_ffn_W_v, "Wo": L0_attn_Wo}
    vectors = {"conv_w": (L0_attn_conv_w, TAPS), "conv_b": (L0_attn_conv_b, 1), "bi": (L0_attn_lru_bi, 1),
               "bg": (L0_attn_lru_bg, 1), "lam": (L0_attn_lam, 1), "mu_r": (L0_ffn_mu_r, 1),
               "mu_k": (L0_ffn_mu_k, 1)}
    wcol, _ = weight_columns(D, H)
    pcol, _ = param_columns(D, H)
    arrays = {
        "x": np.ascontiguousarray(x.reshape(B * S, D)),
        "weights": np.ascontiguousarray(np.concatenate([by_input(matrices[n]) for n in wcol], axis=1)),
        "params": np.ascontiguousarray(np.concatenate([by_channel(*vectors[n]) for n in pcol], axis=1)),
    }
    nc = bacc.Bacc("TRN2", target_bir_lowering=False, num_devices=1)
    args = [nc.dram_tensor(n, a.shape, mybir.dt.from_np(a.dtype), kind="ExternalInput").ap()
            for n, a in arrays.items()]
    args.append(nc.dram_tensor("out", (B * S, D), F32, kind="ExternalOutput").ap())
    hawk_rwkv_block(nc, *args, D, H)
    r = run_bass_kernel_spmd(nc, [arrays], core_ids=[0])
    return r.results[0]["out"].reshape(B, S, D)
```

```python
from contextlib import ExitStack

import concourse.bass as bass
from concourse import mybir

ALU = mybir.AluOpType
ACT = mybir.ActivationFunctionType
F32 = mybir.dt.float32
F32R = mybir.dt.float32r

P = 128
T = 512
TT = T // P
HALF = TT // 2
TAPS = 4
HALO = TAPS - 1
EPS = 1e-5

END_TILES = (0, 2, 3, 4)
PARTS = len(END_TILES) - 1
WARM_UP = 26
LOG1P_TERMS = 9
BIAS_STEPS = 3
SETUP_STEPS = 21


def param_columns(D, H):
    kd, kh = D // P, H // P
    at, out = 0, {}
    for name, n in (("conv_w", kh * TAPS), ("conv_b", kh), ("bi", kh), ("bg", kh), ("lam", kh),
                    ("mu_r", kd), ("mu_k", kd)):
        out[name] = (at, n)
        at += n
    return out, at


def weight_columns(D, H):
    kd, kh = D // P, H // P
    at, out = 0, {}
    for name, k, n in (("Wi", kd, H), ("W_k", kd, D), ("Wg", kd, H), ("W_r", kd, D),
                       ("lru_Wi", kh, H), ("lru_Wg", kh, H), ("W_v", kd, D), ("Wo", kh, D)):
        out[name] = (at, k, n)
        at += k * n
    return out, at


def hawk_rwkv_block(nc: bass.Bass, x: bass.AP, weights: bass.AP, params: bass.AP, out: bass.AP, D, H):
    NTOK = x.shape[0]
    GROUPS = NTOK // T
    SEQS = GROUPS // 2
    KD, KH = D // P, H // P
    PCOL, _ = param_columns(D, H)
    WCOL, WTOTAL = weight_columns(D, H)
    assert T == 512 and KD == 2 and KH == 3 and GROUPS % 2 == 0 and WTOTAL == 4 * KH * T

    x_groups = x.rearrange("(g j p) d -> g p j d", p=P, j=TT)
    out_groups = out.rearrange("(g j p) d -> g p j d", p=P, j=TT)

    with ExitStack() as ctx:
        def sb(name, shape, dt=F32):
            return ctx.enter_context(nc.sbuf_tensor(name, shape, dt))

        def sem(name):
            return ctx.enter_context(nc.semaphore(name))

        def sems(name, n):
            return [sem(f"{name}{k}") for k in range(n)]

        psA = ctx.enter_context(nc.psum_tensor("psA", [P, KH, T], F32))
        psB = ctx.enter_context(nc.psum_tensor("psB", [P, KH, T], F32))
        psC = ctx.enter_context(nc.psum_tensor("psC", [P, KD, T], F32))
        psV = psA[:, 0:KD, :].rearrange("p a (b d) -> p (a b) d", d=D)
        end_psum = [psB[:, 0:2, 0:D], psB[:, 2:3, 0:D], psA[:, 2:3, 0:D]]
        psCt = psC[:, :, :].rearrange("p a (b d) -> p (a b) d", d=D)

        w_hi = sb("w_hi", [P, WTOTAL], F32R)
        w_lo = sb("w_lo", [P, WTOTAL], F32R)
        par = sb("par", [P, params.shape[1]])
        ident = sb("ident", [P, P])
        half_bi = sb("half_bi", [P, KH])
        half_bg = sb("half_bg", [P, KH])
        half_c = sb("half_c", [P, KH])
        full_c = sb("full_c", [P, KH])
        sp = sb("sp", [P, 8, KH])
        beta_bias = sb("beta_bias", [P, 1])
        minus_half = sb("minus_half", [P, TT])

        x_in = [sb(f"x_in{k}", [P, TT, D]) for k in range(2)]
        stats = sb("stats", [P, TT, 6])
        mean_var = sb("mean_var", [P, TT, 2])
        var_eps = sb("var_eps", [P, TT])
        rstd = sb("rstd", [P, TT])
        xn = sb("xn", [P, TT, D])
        tanh_r = sb("tanh_r", [P, TT, D])
        acc = [sb(f"acc{k}", [P, TT, D]) for k in range(2)]

        xt = sb("xt", [P, KD, 1 + T])
        xt_hi = sb("xt_hi", [P, KD, T], F32R)
        xt_lo = sb("xt_lo", [P, KD, T], F32R)
        xk = sb("xk", [P, KD, T])
        xk_hi = sb("xk_hi", [P, KD, T], F32R)
        xk_lo = sb("xk_lo", [P, KD, T], F32R)
        xr = sb("xr", [P, KD, T])
        xr_hi = sb("xr_hi", [P, KD, T], F32R)
        xr_lo = sb("xr_lo", [P, KD, T], F32R)
        ksq = sb("ksq", [P, KD, T])
        ksq_hi = sb("ksq_hi", [P, KD, T], F32R)
        ksq_lo = sb("ksq_lo", [P, KD, T], F32R)
        u = sb("u", [P, KH, HALO + T])
        y = sb("y", [P, KH, T])
        y_hi = sb("y_hi", [P, KH, T], F32R)
        y_lo = sb("y_lo", [P, KH, T], F32R)
        hb = [sb(f"hb{k}", [P, KH, T]) for k in range(2)]
        a2 = sb("a2", [P, KH, T])
        alpha = sb("alpha", [P, KH, T])
        z = [sb(f"z{k}", [P, KH, T]) for k in range(2)]
        z_hi = sb("z_hi", [P, KH, T], F32R)
        z_lo = sb("z_lo", [P, KH, T], F32R)
        h_last = sb("h_last", [P, KH])

        stage = [z[0], z[1], hb[0], hb[1]]
        SLAB = KH * T
        WI_END = WCOL["W_k"][0]
        W_V_COLUMNS = (WCOL["W_v"][0], WCOL["W_v"][0] + WCOL["W_v"][1] * WCOL["W_v"][2])

        def scaled_parts(lo, hi):
            a, b = W_V_COLUMNS
            return [(lo, a, 1.0), (a, b, 0.5), (b, hi, 1.0)] if lo < a < b < hi else [(lo, hi, 1.0)]

        def pcol(name, k=0, n=1):
            at = PCOL[name][0]
            return par[:, at + k:at + k + n]

        def weight(tile, name, k, a, b):
            at, _, n = WCOL[name]
            return tile[:, at + k * n + a:at + k * n + b]

        w_loaded = sems("w_loaded", 4)
        p_loaded = sem("p_loaded")
        wi_hi_ready = sem("wi_hi_ready")
        wi_lo_ready = sem("wi_lo_ready")
        w_hi_ready = sem("w_hi_ready")
        w_lo_ready = sems("w_lo_ready", 4)
        w_v_lo_ready = sem("w_v_lo_ready")
        setup_dve = sem("setup_dve")
        setup_act = sem("setup_act")
        setup_pool = sem("setup_pool")
        x_first = sems("x_first", 2)
        x_loaded = sems("x_loaded", 2)
        out_stored = sems("out_stored", 2)
        stats_ready = sem("stats_ready")
        mean_ready = sem("mean_ready")
        vareps_ready = sem("vareps_ready")
        rstd_ready = sem("rstd_ready")
        xn_first = sems("xn_first", TT)
        xn_ready = sem("xn_ready")
        xt_ready = sem("xt_ready")
        xt_hi_ready = sem("xt_hi_ready")
        xt_taken = sem("xt_taken")
        xt_lo_ready = sem("xt_lo_ready")
        xt_halo = sem("xt_halo")
        diff_ready = sem("diff_ready")
        xk_ready = sems("xk_ready", KD)
        xk_hi_ready = sem("xk_hi_ready")
        xk_lo_ready = sem("xk_lo_ready")
        xr_ready = sems("xr_ready", KD)
        xr_hi_ready = sem("xr_hi_ready")
        xr_lo_ready = sem("xr_lo_ready")
        u_ready = sems("u_ready", KH)
        u_taken = sems("u_taken", KH)
        u_halo = sem("u_halo")
        conv_tap = [sems(f"conv_tap{k}_", KH) for k in range(HALO)]
        y_hi_ready = sems("y_hi_ready", KH)
        y_lo_ready = sem("y_lo_ready")
        k_ready = sem("k_ready")
        k_taken = sem("k_taken")
        ksq_ready = sem("ksq_ready")
        ksq_lo_ready = sem("ksq_lo_ready")
        gate_ready = sem("gate_ready")
        gate_taken = sem("gate_taken")
        r_ready = sem("r_ready")
        r_taken = sem("r_taken")
        ig_ready = sems("ig_ready", KH)
        ig_taken = sems("ig_taken", KH)
        rg_ready = sems("rg_ready", KH)
        rg_taken = sems("rg_taken", KH)
        alpha_ready = sem("alpha_ready")
        beta_ready = sem("beta_ready")
        iy_ready = sem("iy_ready")
        xb_ready = sem("xb_ready")
        h_ready = sem("h_ready")
        h_last_ready = sem("h_last_ready")
        z_ready = sem("z_ready")
        z_hi_ready = sem("z_hi_ready")
        z_lo_ready = sem("z_lo_ready")
        v_ready = sems("v_ready", 2)
        v_taken = sems("v_taken", 2)
        resid_added = sem("resid_added")
        o_ready = sem("o_ready")
        out_ready = sem("out_ready")
        end_alpha = sem("end_alpha")
        end_a2 = sem("end_a2")
        end_beta = sem("end_beta")
        end_xb = sems("end_xb", PARTS)
        end_h = sem("end_h")
        end_z = sem("end_z")
        end_z_hi = sems("end_z_hi", PARTS)
        end_z_lo = sems("end_z_lo", PARTS)
        end_o = sem("end_o")
        end_out = sem("end_out")
        end_stored = sem("end_stored")

        def for_all_groups(eng, step):
            step(0, 0, 0, 0, False)
            step(1, 0, 1, 1, False)
            with eng.Fori(1, SEQS - 1) as seq:
                step(seq * 2, seq, 0, 2, False)
                step(seq * 2 + 1, seq, 1, 2, False)
            step(GROUPS - 2, SEQS - 1, 0, 2, False)
            step(GROUPS - 1, SEQS - 1, 1, 2, True)

        part_tiles = [slice(a, b) for a, b in zip(END_TILES, END_TILES[1:])]
        part_tokens = [slice(t.start * P, t.stop * P) for t in part_tiles]

        def tiles_of_part(n):
            return [slice(j * P, (j + 1) * P) for j in range(END_TILES[n], END_TILES[n + 1])]

        block = ctx.enter_context(nc.Block())

        @block.sync
        def _(sp_eng):
            def load_x(g, odd):
                sp_eng.dma_start(x_in[odd][:, :, :],
                                 x_groups[bass.ds(g, 1)].rearrange("g p j d -> (g p) j d")
                                 ).then_inc(x_loaded[odd], 16)

            def store(g, odd):
                sp_eng.wait_ge(out_ready, g + 1)
                sp_eng.dma_start(out_groups[bass.ds(g, 1)].rearrange("g p j d -> (g p) j d"),
                                 acc[odd][:, :, :]).then_inc(out_stored[odd], 16)

            for n in range(2):
                sp_eng.dma_start(x_in[0][:, n * HALF:(n + 1) * HALF, :],
                                 x_groups[0][:, n * HALF:(n + 1) * HALF, :]).then_inc(x_first[n], 16)
            for k in range(4):
                sp_eng.dma_start(stage[k][:, :, :].rearrange("p a b -> p (a b)"),
                                 weights[:, k * SLAB:(k + 1) * SLAB]).then_inc(w_loaded[k], 16)
            load_x(1, 1)

            def step(g, seq, odd, ago, last):
                if not (isinstance(g, int) and g + 2 >= GROUPS):
                    sp_eng.wait_ge(resid_added, g + 1)
                    load_x(g + 2, odd)
                if ago:
                    store(g - 1, 1 - odd)

            for_all_groups(sp_eng, step)
            for n, tiles in enumerate(part_tiles):
                sp_eng.wait_ge(end_out, n + 1)
                sp_eng.dma_start(out_groups[GROUPS - 1][:, tiles, :], acc[1][:, tiles, :]).then_inc(end_stored, 16)
            sp_eng.wait_ge(out_stored[0], 16 * SEQS)
            sp_eng.wait_ge(out_stored[1], 16 * (SEQS - 1))
            sp_eng.wait_ge(end_stored, 16 * PARTS)

        @block.tensor
        def _(pe):
            def product(dst, name, m, rhs_hi, rhs_lo, lo_sem, count):
                _, K, _ = WCOL[name]
                a, b = m * P, (m + 1) * P
                for k in range(K):
                    nc.tensor.matmul(dst, weight(w_hi, name, k, a, b), rhs_hi[:, k, :], start=(k == 0), stop=False)
                    nc.tensor.matmul(dst, weight(w_lo, name, k, a, b), rhs_hi[:, k, :], start=False, stop=False)
                if lo_sem is not None:
                    pe.wait_ge(lo_sem, count)
                for k in range(K):
                    mm = nc.tensor.matmul(dst, weight(w_hi, name, k, a, b), rhs_lo[:, k, :],
                                          start=False, stop=(k == K - 1))
                return mm

            def product_by_token(dst, name, lhs_hi, lhs_lo, tiles=range(TT)):
                _, K, n = WCOL[name]
                for i, j in enumerate(tiles):
                    t = slice(j * P, (j + 1) * P)
                    for k in range(K):
                        nc.tensor.matmul(dst[:, i, :], lhs_hi[:, k, t], weight(w_hi, name, k, 0, n),
                                         start=(k == 0), stop=False)
                        nc.tensor.matmul(dst[:, i, :], lhs_hi[:, k, t], weight(w_lo, name, k, 0, n),
                                         start=False, stop=False)
                    for k in range(K):
                        mm = nc.tensor.matmul(dst[:, i, :], lhs_lo[:, k, t], weight(w_hi, name, k, 0, n),
                                              start=False, stop=(k == K - 1))
                return mm

            def transpose_input(g, first):
                if not first:
                    pe.wait_ge(xn_ready, g)
                    pe.wait_ge(r_taken, g)
                for j in range(TT):
                    if first:
                        pe.wait_ge(xn_first[j], 1)
                    for k in range(KD):
                        mm = nc.tensor.transpose(psC[:, k, j * P:(j + 1) * P], xn[:, j, k * P:(k + 1) * P],
                                                 ident[:, :])
                mm.then_inc(xt_ready, 1)

            def project(g):
                pe.wait_ge(z_hi_ready, g + 1)
                pe.wait_ge(z_lo_ready, g + 1)
                product_by_token(psCt, "Wo", z_hi, z_lo).then_inc(o_ready, 1)

            pe.wait_ge(setup_pool, 2)
            for _ in range(WARM_UP):
                nc.tensor.transpose(psA[:, 0, 0:P], ident[:, :], ident[:, :])
            transpose_input(0, True)

            def step(g, seq, odd, ago, last):
                if not ago:
                    pe.wait_ge(wi_lo_ready, 1)
                pe.wait_ge(xt_hi_ready, g + 1)
                if ago:
                    pe.wait_ge(ig_taken[KH - 1], g)
                for c in range(KH):
                    if ago and c < 2:
                        pe.wait_ge(v_taken[c], g)
                    product(psA[:, c, :], "Wi", c, xt_hi, xt_lo, xt_lo_ready if c == 0 else None, g + 1
                            ).then_inc(u_ready[c], 1)
                if not ago:
                    pe.wait_ge(w_lo_ready[0], 1)
                pe.wait_ge(xk_hi_ready, g + 1)
                if ago >= 2:
                    pe.wait_ge(out_ready, g - 1)
                for c in range(KD):
                    mm = product(psC[:, c, :], "W_k", c, xk_hi, xk_lo, xk_lo_ready if c == 0 else None, g + 1)
                mm.then_inc(k_ready, 1)
                if not ago:
                    pe.wait_ge(w_lo_ready[1], 1)
                if ago:
                    pe.wait_ge(rg_taken[KH - 1], g)
                for c in range(KH):
                    mm = product(psB[:, c, :], "Wg", c, xt_hi, xt_lo, None, 0)
                mm.then_inc(gate_ready, 1)
                pe.wait_ge(xr_hi_ready, g + 1)
                pe.wait_ge(xr_lo_ready, g + 1)
                pe.wait_ge(k_taken, g + 1)
                product_by_token(psCt, "W_r", xr_hi, xr_lo).then_inc(r_ready, 1)
                if not ago:
                    pe.wait_ge(w_lo_ready[2], 1)
                for c in range(KH):
                    pe.wait_ge(y_hi_ready[c], g + 1)
                    pe.wait_ge(u_taken[c], g + 1)
                for c in range(KH):
                    product(psA[:, c, :], "lru_Wi", c, y_hi, y_lo, y_lo_ready if c == 0 else None, g + 1
                            ).then_inc(ig_ready[c], 1)
                if not last:
                    transpose_input(g + 1, False)
                if not ago:
                    pe.wait_ge(w_lo_ready[3], 1)
                pe.wait_ge(gate_taken, g + 1)
                for c in range(KH):
                    product(psB[:, c, :], "lru_Wg", c, y_hi, y_lo, None, 0).then_inc(rg_ready[c], 1)
                if not ago:
                    pe.wait_ge(w_v_lo_ready, 1)
                pe.wait_ge(ksq_lo_ready, g + 1)
                pe.wait_ge(ig_taken[KD - 1], g + 1)
                for n in range(2):
                    product_by_token(psV[:, n * HALF:(n + 1) * HALF, :], "W_v", ksq_hi, ksq_lo,
                                     range(n * HALF, (n + 1) * HALF)
                                     ).then_inc(v_ready[n], 1)
                if ago:
                    if last:
                        pe.wait_ge(r_taken, g + 1)
                    else:
                        pe.wait_ge(xt_taken, g + 2)
                    project(g - 1)

            for_all_groups(pe, step)
            pe.wait_ge(rg_taken[KH - 1], GROUPS)

            def end_hi_passes(n):
                _, K, w = WCOL["Wo"]
                pe.wait_ge(end_z_hi[n], 1)
                for i, t in enumerate(tiles_of_part(n)):
                    for k in range(K):
                        nc.tensor.matmul(end_psum[n][:, i, :], z_hi[:, k, t], weight(w_hi, "Wo", k, 0, w),
                                         start=(k == 0), stop=False)
                        nc.tensor.matmul(end_psum[n][:, i, :], z_hi[:, k, t], weight(w_lo, "Wo", k, 0, w),
                                         start=False, stop=False)

            def end_lo_passes(n):
                _, K, w = WCOL["Wo"]
                pe.wait_ge(end_z_lo[n], 1)
                for i, t in enumerate(tiles_of_part(n)):
                    for k in range(K):
                        mm = nc.tensor.matmul(end_psum[n][:, i, :], z_lo[:, k, t], weight(w_hi, "Wo", k, 0, w),
                                              start=False, stop=(k == K - 1))
                mm.then_inc(end_o, 1)

            end_hi_passes(0)
            for n in range(PARTS):
                if n + 1 < PARTS:
                    end_hi_passes(n + 1)
                end_lo_passes(n)

        @block.scalar
        def _(act):
            def round_weights(k):
                act.wait_ge(w_loaded[k], 16)
                lo, hi = k * SLAB, (k + 1) * SLAB
                raw = stage[k][:, :, :].rearrange("p a b -> p (a b)")
                if k == 0:
                    nc.scalar.activation(w_hi[:, 0:WI_END], raw[:, 0:WI_END], ACT.Copy).then_inc(wi_hi_ready, 1)
                    lo = WI_END
                for a, b, scale in scaled_parts(lo, hi):
                    last = nc.scalar.activation(w_hi[:, a:b], raw[:, a - k * SLAB:b - k * SLAB], ACT.Copy,
                                                scale=scale)
                last.then_inc(w_hi_ready, 1)

            act.dma_start(par[:, :], params).then_inc(p_loaded, 16)
            act.wait_ge(setup_dve, 1)
            nc.scalar.activation(sp[:, 1, :], sp[:, 0, :], ACT.Exp).then_inc(setup_act, 1)
            round_weights(0)

            def take_transposed(g, first):
                act.wait_ge(xt_ready, g + 1)
                act.wait_ge(xt_halo, g + 1)
                if not first:
                    act.wait_ge(gate_ready, g)
                nc.scalar.activation(xt_hi[:, :, :], psC[:, :, :], ACT.Copy).then_inc(xt_hi_ready, 1)
                nc.scalar.activation(xt[:, :, 1:1 + T], psC[:, :, :], ACT.Copy).then_inc(xt_taken, 1)

            def make_beta(g):
                act.wait_ge(alpha_ready, g + 1)
                nc.scalar.activation(a2[:, :, :], a2[:, :, :], ACT.Sqrt, bias=beta_bias[:, 0:1],
                                     scale=-0.25 * (1 - 2.0 ** -24)).then_inc(beta_ready, 1)

            def round_z(g, odd, first):
                act.wait_ge(z_ready, g + 1)
                if not first:
                    act.wait_ge(o_ready, g)
                nc.scalar.activation(z_hi[:, :, :], z[odd][:, :, :], ACT.Copy).then_inc(z_hi_ready, 1)

            take_transposed(0, True)
            for k in range(1, 4):
                round_weights(k)

            def step(g, seq, odd, ago, last):
                act.wait_ge(u_halo, g + 1)
                if ago:
                    act.wait_ge(iy_ready, g)
                for c in range(KH):
                    act.wait_ge(u_ready[c], g + 1)
                    nc.scalar.activation(u[:, c, HALO:HALO + T], psA[:, c, :], ACT.Copy)
                    nc.scalar.activation(y[:, c, :], psA[:, c, :], ACT.Identity,
                                         scale=pcol("conv_w", c * TAPS + HALO), bias=pcol("conv_b", c)
                                         ).then_inc(u_taken[c], 1)
                act.wait_ge(k_ready, g + 1)
                if ago:
                    act.wait_ge(ksq_lo_ready, g)
                nc.scalar.activation(ksq[:, :, :], psC[:, :, :], ACT.Relu).then_inc(k_taken, 1)
                act.wait_ge(k_taken, g + 1)
                if ago:
                    act.wait_ge(v_ready[1], g)
                nc.scalar.activation(ksq_hi[:, :, :], ksq[:, :, :], ACT.Square)
                nc.scalar.activation(ksq[:, :, :], ksq[:, :, :], ACT.Square).then_inc(ksq_ready, 1)
                if ago == 1:
                    make_beta(0)
                act.wait_ge(gate_ready, g + 1)
                if not ago:
                    act.wait_ge(wi_lo_ready, 1)
                    act.wait_ge(w_lo_ready[0], 1)
                elif ago >= 2:
                    act.wait_ge(z_lo_ready, g - 1)
                else:
                    act.wait_ge(w_lo_ready[1], 1)
                nc.scalar.activation(z[odd][:, :, :], psB[:, :, :], ACT.Gelu).then_inc(gate_taken, 1)
                act.wait_ge(r_ready, g + 1)
                if ago:
                    act.wait_ge(v_taken[1], g)
                nc.scalar.activation(tanh_r[:, :, :], psCt, ACT.Tanh, scale=0.5).then_inc(r_taken, 1)
                if ago >= 2:
                    act.wait_ge(z_ready, g - 1)
                elif ago:
                    act.wait_ge(w_lo_ready[3], 1)
                    act.wait_ge(w_v_lo_ready, 1)
                else:
                    act.wait_ge(w_lo_ready[2], 1)
                for c in range(KH):
                    act.wait_ge(ig_ready[c], g + 1)
                    nc.scalar.activation(hb[odd][:, c, :], psA[:, c, :], ACT.Tanh, scale=0.5,
                                         bias=half_bi[:, c:c + 1]).then_inc(ig_taken[c], 1)
                if not last:
                    take_transposed(g + 1, False)
                if ago:
                    round_z(g - 1, 1 - odd, ago < 2)
                    act.wait_ge(h_ready, g)
                if not ago:
                    act.wait_ge(setup_dve, SETUP_STEPS)
                for c in range(KH):
                    act.wait_ge(rg_ready[c], g + 1)
                    nc.scalar.activation(a2[:, c, :], psB[:, c, :], ACT.Tanh, scale=0.5,
                                         bias=half_bg[:, c:c + 1]).then_inc(rg_taken[c], 1)
                    act.wait_ge(rg_taken[c], g + 1)
                    e = nc.scalar.activation(alpha[:, c, :], a2[:, c, :], ACT.Exp, scale=half_c[:, c:c + 1],
                                             bias=half_c[:, c:c + 1])
                    if last:
                        e.then_inc(end_alpha, 1)
                    else:
                        e = nc.scalar.activation(a2[:, c, :], a2[:, c, :], ACT.Exp, scale=full_c[:, c:c + 1],
                                                 bias=full_c[:, c:c + 1])
                if not last:
                    e.then_inc(alpha_ready, 1)
                    if ago:
                        make_beta(g)

            act.wait_ge(setup_dve, BIAS_STEPS)
            act.wait_ge(setup_pool, 4)
            for_all_groups(act, step)
            act.wait_ge(end_a2, KH)
            for t in part_tokens:
                nc.scalar.activation(a2[:, :, t], a2[:, :, t], ACT.Sqrt, bias=beta_bias[:, 0:1],
                                     scale=-0.25 * (1 - 2.0 ** -24)).then_inc(end_beta, 1)
            act.wait_ge(o_ready, GROUPS - 1)
            for n, t in enumerate(part_tokens[:-1]):
                act.wait_ge(end_z, n + 1)
                nc.scalar.activation(z_hi[:, :, t], z[1][:, :, t], ACT.Copy).then_inc(end_z_hi[n], 1)

        @block.vector
        def _(dve):
            done = [0]

            def after(ins):
                done[0] += 1
                ins.then_inc(setup_dve, 1)
                dve.wait_ge(setup_dve, done[0])

            V = nc.vector

            def stats_of(g, seq, odd, first=False):
                if not first:
                    dve.wait_ge(x_loaded[odd], (seq + odd) * 16)
                for j in range(TT):
                    if first and j % HALF == 0:
                        dve.wait_ge(x_first[j // HALF], 16)
                    e = V.bn_stats(stats[:, j, :], x_in[odd][:, j, :])
                e.then_inc(stats_ready, 1)

            def aggregate(g):
                for j in range(TT):
                    e = V.bn_aggr(mean_var[:, j, :], stats[:, j, :])
                e.then_inc(mean_ready, 1)
                dve.wait_ge(mean_ready, g + 1)
                V.tensor_scalar(var_eps[:, :], mean_var[:, :, 1], EPS, None, ALU.add).then_inc(vareps_ready, 1)

            def normalise(g, odd, first):
                dve.wait_ge(rstd_ready, g + 1)
                if not first:
                    dve.wait_ge(xt_ready, g)
                for j in range(TT):
                    e = V.tensor_scalar(xn[:, j, :], x_in[odd][:, j, :], mean_var[:, j, 0:1], rstd[:, j:j + 1],
                                        ALU.subtract, ALU.mult)
                    if first:
                        e.then_inc(xn_first[j], 1)
                    elif j == TT - 1:
                        e.then_inc(xn_ready, 1)

            def set_xt_halo(odd):
                if odd:
                    V.tensor_copy(xt[:, :, 0:1], xt[:, :, T:T + 1]).then_inc(xt_halo, 1)
                else:
                    V.memset(xt[:, :, 0:1], 0.0).then_inc(xt_halo, 1)

            def set_u_halo(odd):
                if odd:
                    V.tensor_copy(u[:, :, 0:HALO], u[:, :, T:T + HALO]).then_inc(u_halo, 1)
                else:
                    V.memset(u[:, :, 0:HALO], 0.0).then_inc(u_halo, 1)

            def begin_mix(g, first):
                dve.wait_ge(xt_taken, g + 1)
                V.tensor_tensor(xt_lo[:, :, :], xt[:, :, 1:1 + T], xt_hi[:, :, :].bitcast(F32), ALU.subtract
                                ).then_inc(xt_lo_ready, 1)
                if not first:
                    dve.wait_ge(xr_lo_ready, g)
                V.tensor_tensor(xr[:, :, :], xt[:, :, 1:1 + T], xt[:, :, 0:T], ALU.subtract).then_inc(diff_ready, 1)
                dve.wait_ge(diff_ready, g + 1)
                if not first:
                    dve.wait_ge(xk_lo_ready, g)
                for k in range(KD):
                    V.scalar_tensor_tensor(out=xk[:, k, :], in0=xr[:, k, :], scalar=pcol("mu_k", k),
                                           in1=xt[:, k, 0:T], op0=ALU.mult, op1=ALU.add).then_inc(xk_ready[k], 1)

            def mix(g, odd, first, split_here):
                if not first:
                    dve.wait_ge(k_ready, g)
                for k in range(KD):
                    dve.wait_ge(xk_ready[k], g + 1)
                V.tensor_copy(xk_hi[:, :, :], xk[:, :, :]).then_inc(xk_hi_ready, 1)
                if split_here:
                    dve.wait_ge(xk_hi_ready, g + 1)
                    V.tensor_tensor(xk_lo[:, :, :], xk[:, :, :], xk_hi[:, :, :].bitcast(F32), ALU.subtract
                                    ).then_inc(xk_lo_ready, 1)
                for k in range(KD):
                    V.scalar_tensor_tensor(out=xr[:, k, :], in0=xr[:, k, :], scalar=pcol("mu_r", k),
                                           in1=xt[:, k, 0:T], op0=ALU.mult, op1=ALU.add).then_inc(xr_ready[k], 1)
                if not first:
                    dve.wait_ge(r_ready, g)
                for k in range(KD):
                    dve.wait_ge(xr_ready[k], g + 1)
                V.tensor_copy(xr_hi[:, :, :], xr[:, :, :]).then_inc(xr_hi_ready, 1)
                set_xt_halo(1 - odd)

            def convolve_tap(g, tap):
                for c in range(KH):
                    if tap == HALO - 1:
                        dve.wait_ge(u_taken[c], g + 1)
                    else:
                        dve.wait_ge(conv_tap[tap + 1][c], g + 1)
                    V.scalar_tensor_tensor(out=y[:, c, :], in0=u[:, c, tap:tap + T],
                                           scalar=pcol("conv_w", c * TAPS + tap), in1=y[:, c, :],
                                           op0=ALU.mult, op1=ALU.add).then_inc(conv_tap[tap][c], 1)

            def gate_input(g, odd):
                dve.wait_ge(beta_ready, g + 1)
                dve.wait_ge(iy_ready, g + 1)
                V.tensor_tensor(hb[odd][:, :, :], hb[odd][:, :, :], a2[:, :, :], ALU.mult).then_inc(xb_ready, 1)

            def recur(g, seq, odd):
                dve.wait_ge(xb_ready, g + 1)
                if odd:
                    dve.wait_ge(h_last_ready, seq + 1)
                for c in range(KH):
                    e = V.tensor_tensor_scan(hb[odd][:, c, :], alpha[:, c, :], hb[odd][:, c, :],
                                             h_last[:, c:c + 1] if odd else 0.0, ALU.mult, ALU.add)
                e.then_inc(h_ready, 1)
                dve.wait_ge(h_ready, g + 1)
                if not odd:
                    V.tensor_copy(h_last[:, :], hb[odd][:, :, T - 1]).then_inc(h_last_ready, 1)
                dve.wait_ge(gate_taken, g + 1)
                V.tensor_tensor(z[odd][:, :, :], z[odd][:, :, :], hb[odd][:, :, :], ALU.mult).then_inc(z_ready, 1)

            def finish(g, odd):
                dve.wait_ge(o_ready, g + 1)
                dve.wait_ge(resid_added, g + 1)
                V.tensor_tensor(acc[odd][:, :, :], psCt, acc[odd][:, :, :], ALU.add).then_inc(out_ready, 1)

            def log1p_terms(lo, hi):
                for n in range(hi, lo - 1, -1):
                    if n == LOG1P_TERMS:
                        after(V.tensor_scalar(sp[:, 6, :], sp[:, 5, :], 1.0 / (2 * n + 1), None, ALU.mult))
                    else:
                        after(V.scalar_tensor_tensor(out=sp[:, 6, :], in0=sp[:, 6, :], scalar=1.0 / (2 * n + 1),
                                                     in1=sp[:, 5, :], op0=ALU.add, op1=ALU.mult))

            def begin_decay():
                dve.wait_ge(setup_act, 1)
                after(V.tensor_scalar(sp[:, 2, :], sp[:, 1, :], 2.0, None, ALU.add))
                after(V.reciprocal(sp[:, 3, :], sp[:, 2, :]))
                after(V.tensor_tensor(sp[:, 4, :], sp[:, 1, :], sp[:, 3, :], ALU.mult))
                after(V.tensor_tensor(sp[:, 5, :], sp[:, 4, :], sp[:, 4, :], ALU.mult))

            def end_decay():
                log1p_terms(1, LOG1P_TERMS)
                after(V.scalar_tensor_tensor(out=sp[:, 7, :], in0=sp[:, 6, :], scalar=1.0, in1=sp[:, 4, :],
                                             op0=ALU.add, op1=ALU.mult))
                after(V.tensor_scalar(sp[:, 6, :], lam, 0.0, None, ALU.max))
                after(V.scalar_tensor_tensor(out=sp[:, 2, :], in0=sp[:, 7, :], scalar=2.0, in1=sp[:, 6, :],
                                             op0=ALU.mult, op1=ALU.add))
                after(V.tensor_scalar(half_c[:, :], sp[:, 2, :], -4.0, None, ALU.mult))
                after(V.tensor_scalar(full_c[:, :], sp[:, 2, :], -8.0, None, ALU.mult))
                assert done[0] == SETUP_STEPS

            def split_weights(k, a, b, scale, ready):
                raw = stage[k][:, :, :].rearrange("p a b -> p (a b)")
                V.scalar_tensor_tensor(out=w_lo[:, a:b], in0=raw[:, a - k * SLAB:b - k * SLAB], scalar=scale,
                                       in1=w_hi[:, a:b].bitcast(F32), op0=ALU.mult, op1=ALU.subtract
                                       ).then_inc(ready, 1)

            set_xt_halo(0)
            set_u_halo(0)
            dve.wait_ge(p_loaded, 16)
            lam = pcol("lam", 0, KH)
            after(V.scalar_tensor_tensor(out=sp[:, 0, :], in0=lam, scalar=-1.0, in1=lam, op0=ALU.mult, op1=ALU.min))
            stats_of(0, 0, 0, first=True)
            dve.wait_ge(stats_ready, 1)
            aggregate(0)
            after(V.tensor_scalar(half_bi[:, :], pcol("bi", 0, KH), 0.5, None, ALU.mult))
            after(V.tensor_scalar(half_bg[:, :], pcol("bg", 0, KH), 0.5, None, ALU.mult))
            assert done[0] == BIAS_STEPS
            begin_decay()
            normalise(0, 0, True)
            dve.wait_ge(wi_hi_ready, 1)
            split_weights(0, 0, WI_END, 1.0, wi_lo_ready)
            begin_mix(0, True)
            mix(0, 0, True, True)

            def step(g, seq, odd, ago, last):
                convolve_tap(g, 2)
                if ago and not last:
                    stats_of(g + 1, seq + odd, 1 - odd)
                convolve_tap(g, 1)
                convolve_tap(g, 0)
                if ago:
                    dve.wait_ge(rg_ready[KH - 1], g)
                for c in range(KH):
                    dve.wait_ge(conv_tap[0][c], g + 1)
                    V.tensor_copy(y_hi[:, c, :], y[:, c, :]).then_inc(y_hi_ready[c], 1)
                if ago and not last:
                    dve.wait_ge(stats_ready, g + 2)
                for c in range(KH):
                    dve.wait_ge(y_hi_ready[c], g + 1)
                    e = V.tensor_tensor(y_lo[:, c, :], y[:, c, :], y_hi[:, c, :].bitcast(F32), ALU.subtract)
                e.then_inc(y_lo_ready, 1)
                if not ago:
                    stats_of(g + 1, seq + odd, 1 - odd)
                    dve.wait_ge(stats_ready, g + 2)
                if not last:
                    set_u_halo(1 - odd)
                    aggregate(g + 1)
                if not ago:
                    dve.wait_ge(w_hi_ready, 4)
                    split_weights(3, *W_V_COLUMNS, 0.5, w_v_lo_ready)
                if ago:
                    gate_input(g - 1, 1 - odd)
                if not last:
                    normalise(g + 1, 1 - odd, False)
                if ago:
                    recur(g - 1, seq + (odd - 1), 1 - odd)
                else:
                    end_decay()
                dve.wait_ge(ig_taken[KH - 1], g + 1)
                V.scalar_tensor_tensor(out=hb[odd][:, :, :], in0=hb[odd][:, :, :], scalar=1.0, in1=y[:, :, :],
                                       op0=ALU.add, op1=ALU.mult).then_inc(iy_ready, 1)
                if last:
                    for c in range(KH):
                        dve.wait_ge(end_alpha, c + 1)
                        V.tensor_tensor(a2[:, c, :], alpha[:, c, :], alpha[:, c, :], ALU.mult).then_inc(end_a2, 1)
                else:
                    begin_mix(g + 1, False)
                    if ago:
                        mix(g + 1, 1 - odd, False, False)
                dve.wait_ge(r_taken, g + 1)
                if ago >= 2:
                    dve.wait_ge(out_stored[odd], seq * 16)
                for n in range(2):
                    tiles = slice(n * HALF, (n + 1) * HALF)
                    dve.wait_ge(v_ready[n], g + 1)
                    V.scalar_tensor_tensor(out=acc[odd][:, tiles, :], in0=tanh_r[:, tiles, :], scalar=1.0,
                                           in1=psV[:, tiles, :], op0=ALU.add, op1=ALU.mult
                                           ).then_inc(v_taken[n], 1)
                if not ago:
                    mix(g + 1, 1 - odd, False, True)
                elif not last:
                    finish(g - 1, 1 - odd)

            for_all_groups(dve, step)
            dve.wait_ge(h_last_ready, SEQS)
            dve.wait_ge(iy_ready, GROUPS)
            dve.wait_ge(gate_taken, GROUPS)
            for n, t in enumerate(part_tokens):
                if n == 0:
                    dve.wait_ge(end_beta, 1)
                    V.tensor_tensor(hb[1][:, :, t], hb[1][:, :, t], a2[:, :, t], ALU.mult).then_inc(end_xb[0], 1)
                dve.wait_ge(end_xb[n], 1)
                for c in range(KH):
                    before = hb[1][:, c, t.start - 1:t.start] if n else h_last[:, c:c + 1]
                    e = V.tensor_tensor_scan(hb[1][:, c, t], alpha[:, c, t], hb[1][:, c, t], before,
                                             ALU.mult, ALU.add)
                e.then_inc(end_h, 1)
                dve.wait_ge(end_h, n + 1)
                V.tensor_tensor(z[1][:, :, t], z[1][:, :, t], hb[1][:, :, t], ALU.mult).then_inc(end_z, 1)
                if n == 1:
                    finish(GROUPS - 2, 0)
            dve.wait_ge(end_z, PARTS)
            dve.wait_ge(o_ready, GROUPS - 1)
            V.tensor_copy(z_hi[:, :, t], z[1][:, :, t]).then_inc(end_z_hi[PARTS - 1], 1)
            dve.wait_ge(end_z_hi[PARTS - 1], 1)
            V.tensor_tensor(z_lo[:, :, t], z[1][:, :, t], z_hi[:, :, t].bitcast(F32), ALU.subtract
                            ).then_inc(end_z_lo[PARTS - 1], 1)
            dve.wait_ge(resid_added, GROUPS)
            for n, tiles in enumerate(part_tiles):
                dve.wait_ge(end_o, n + 1)
                V.tensor_tensor(acc[1][:, tiles, :], end_psum[n], acc[1][:, tiles, :], ALU.add
                                ).then_inc(end_out, 1)

        @block.gpsimd
        def _(pool):
            G = nc.gpsimd
            G.memset(ident[:, :], 0.0).then_inc(setup_pool, 1)
            pool.wait_ge(setup_pool, 1)
            G.affine_select(out=ident[:, :], in_=ident[:, :], compare_op=ALU.not_equal, fill=1.0, base=0,
                            pattern=[[-1, P]], channel_multiplier=1).then_inc(setup_pool, 1)
            G.memset(minus_half[:, :], -0.5).then_inc(setup_pool, 1)
            G.memset(beta_bias[:, :], 0.25 * (1 + 2.0 ** -20)).then_inc(setup_pool, 1)

            def inverse_std(g, first):
                pool.wait_ge(vareps_ready, g + 1)
                if first:
                    pool.wait_ge(setup_pool, 3)
                else:
                    pool.wait_ge(xt_ready, g)
                G.tensor_tensor(rstd[:, :], var_eps[:, :], minus_half[:, :], ALU.pow).then_inc(rstd_ready, 1)

            def split_xk(g):
                pool.wait_ge(xk_hi_ready, g + 1)
                pool.wait_ge(k_ready, g)
                G.tensor_tensor(xk_lo[:, :, :], xk[:, :, :], xk_hi[:, :, :].bitcast(F32), ALU.subtract
                                ).then_inc(xk_lo_ready, 1)

            def split_xr(g, first):
                pool.wait_ge(xr_hi_ready, g + 1)
                if not first:
                    pool.wait_ge(r_ready, g)
                G.tensor_tensor(xr_lo[:, :, :], xr[:, :, :], xr_hi[:, :, :].bitcast(F32), ALU.subtract
                                ).then_inc(xr_lo_ready, 1)

            def add_residual(g, odd):
                pool.wait_ge(v_taken[1], g + 1)
                G.tensor_tensor(acc[odd][:, :, :], acc[odd][:, :, :], x_in[odd][:, :, :], ALU.add
                                ).then_inc(resid_added, 1)

            def split_z(g, odd, first):
                pool.wait_ge(z_hi_ready, g + 1)
                if not first:
                    pool.wait_ge(o_ready, g)
                G.tensor_tensor(z_lo[:, :, :], z[odd][:, :, :], z_hi[:, :, :].bitcast(F32), ALU.subtract
                                ).then_inc(z_lo_ready, 1)

            inverse_std(0, True)
            for k in range(4):
                pool.wait_ge(w_hi_ready, k + 1)
                raw = stage[k][:, :, :].rearrange("p a b -> p (a b)")
                for a, b, scale in scaled_parts(k * SLAB if k else WI_END, (k + 1) * SLAB):
                    if scale == 1.0:
                        e = G.tensor_tensor(w_lo[:, a:b], raw[:, a - k * SLAB:b - k * SLAB],
                                            w_hi[:, a:b].bitcast(F32), ALU.subtract)
                e.then_inc(w_lo_ready[k], 1)
                if k == 1:
                    split_xr(0, True)

            def step(g, seq, odd, ago, last):
                if not last:
                    inverse_std(g + 1, False)
                pool.wait_ge(ksq_ready, g + 1)
                G.tensor_tensor(ksq_lo[:, :, :], ksq[:, :, :], ksq_hi[:, :, :].bitcast(F32), ALU.subtract
                                ).then_inc(ksq_lo_ready, 1)
                if ago:
                    split_z(g - 1, 1 - odd, ago < 2)
                if ago and not last:
                    split_xk(g + 1)
                if not last:
                    add_residual(g, odd)
                    split_xr(g + 1, False)

            for_all_groups(pool, step)
            add_residual(GROUPS - 1, 1)
            for n, t in enumerate(part_tokens[1:], start=1):
                pool.wait_ge(end_beta, n + 1)
                pool.wait_ge(iy_ready, GROUPS)
                G.tensor_tensor(hb[1][:, :, t], hb[1][:, :, t], a2[:, :, t], ALU.mult).then_inc(end_xb[n], 1)
            pool.wait_ge(o_ready, GROUPS - 1)
            for n, t in enumerate(part_tokens[:-1]):
                pool.wait_ge(end_z_hi[n], 1)
                G.tensor_tensor(z_lo[:, :, t], z[1][:, :, t], z_hi[:, :, t].bitcast(F32), ALU.subtract
                                ).then_inc(end_z_lo[n], 1)



def kernel(L0_attn_x, L0_attn_Wg, L0_attn_Wi, L0_attn_conv_w, L0_attn_conv_b, L0_attn_lru_Wi, L0_attn_lru_bi,
           L0_attn_lru_Wg, L0_attn_lru_bg, L0_attn_lam, L0_attn_Wo, L0_ffn_W_r, L0_ffn_W_k, L0_ffn_W_v,
           L0_ffn_mu_r, L0_ffn_mu_k):
    import numpy as np
    import concourse.bacc as bacc
    from concourse.bass_utils import run_bass_kernel_spmd

    x = np.asarray(L0_attn_x)
    B, S, D = x.shape
    H = np.asarray(L0_attn_Wg).shape[0]

    def by_input(w):
        w = np.asarray(w)
        return w.T.reshape(w.shape[1] // P, P, w.shape[0]).transpose(1, 0, 2).reshape(P, -1)

    def by_channel(v, n):
        return np.asarray(v).reshape(-1, P, n).transpose(1, 0, 2).reshape(P, -1)

    matrices = {"Wi": L0_attn_Wi, "W_k": L0_ffn_W_k, "Wg": L0_attn_Wg, "W_r": L0_ffn_W_r,
                "lru_Wi": L0_attn_lru_Wi, "lru_Wg": L0_attn_lru_Wg, "W_v": L0_ffn_W_v, "Wo": L0_attn_Wo}
    vectors = {"conv_w": (L0_attn_conv_w, TAPS), "conv_b": (L0_attn_conv_b, 1), "bi": (L0_attn_lru_bi, 1),
               "bg": (L0_attn_lru_bg, 1), "lam": (L0_attn_lam, 1), "mu_r": (L0_ffn_mu_r, 1),
               "mu_k": (L0_ffn_mu_k, 1)}
    wcol, _ = weight_columns(D, H)
    pcol, _ = param_columns(D, H)
    arrays = {
        "x": np.ascontiguousarray(x.reshape(B * S, D)),
        "weights": np.ascontiguousarray(np.concatenate([by_input(matrices[n]) for n in wcol], axis=1)),
        "params": np.ascontiguousarray(np.concatenate([by_channel(*vectors[n]) for n in pcol], axis=1)),
    }
    nc = bacc.Bacc("TRN2", target_bir_lowering=False, num_devices=1)
    args = [nc.dram_tensor(n, a.shape, mybir.dt.from_np(a.dtype), kind="ExternalInput").ap()
            for n, a in arrays.items()]
    args.append(nc.dram_tensor("out", (B * S, D), F32, kind="ExternalOutput").ap())
    hawk_rwkv_block(nc, *args, D, H)
    r = run_bass_kernel_spmd(nc, [arrays], core_ids=[0])
    return r.results[0]["out"].reshape(B, S, D)
```
